# Optimizing a Trainium2 kernel written in Bass

```python
import numpy as np
import jax
import jax.numpy as jnp

def _softmax(x, axis=-1):
    return jax.nn.softmax(x, axis=axis)

def _gelu(x):
    return jax.nn.gelu(x, approximate=True)

def _silu(x):
    return jax.nn.silu(x)

def _sigmoid(x):
    return jax.nn.sigmoid(x)

def _layernorm(x, axis=-1, eps=1e-05):
    m = jnp.mean(x, axis=axis, keepdims=True)
    v = jnp.var(x, axis=axis, keepdims=True)
    return (x - m) / jnp.sqrt(v + eps)

def _scatter_add(tgt, idx, src, axis=0):
    return tgt.at[idx].add(src)

def _segment_sum(src, seg, n):
    return jax.ops.segment_sum(src, seg, n)
kernel_name = 'mk_cond_resid_d4_seqx_r4_8e9143'

def setup_inputs(seed: int=0):
    np.random.seed(seed)
    _w = jnp.asarray

    def _rec_inputs():
        import jax
        import jax.numpy as jnp
        _rk = jax.random.key(seed)
        x = -0.0003929 + 0.9999 * jax.random.normal(jax.random.fold_in(_rk, 1), (16, 256, 256), jnp.float32)
        _lenS = 256 - jax.random.randint(jax.random.fold_in(_rk, 7), (16,), 0, max(1, 256 // 4) + 1, jnp.int32)
        _lenS2 = 256 - jax.random.randint(jax.random.fold_in(_rk, 8), (16,), 0, max(1, 256 // 4) + 1, jnp.int32)
        itok_B_0_7 = jax.random.randint(jax.random.fold_in(_rk, 11), (16,), 0, 8, jnp.int32)
        condB_zX = jax.random.uniform(jax.random.fold_in(_rk, 12), (16,), jnp.float32, 0.0, 0.983423)
        condB_zY = jax.random.uniform(jax.random.fold_in(_rk, 13), (16,), jnp.float32, 0.0, 0.979075)
        condB_zR = jax.random.uniform(jax.random.fold_in(_rk, 14), (16,), jnp.float32, 0.0, 0.9968)
        fside_BxSxS_0 = 4.13588e-05 + 0.999923 * jax.random.normal(jax.random.fold_in(_rk, 15), (16, 256, 256), jnp.float32)
        itok_B_18_1004 = jax.random.randint(jax.random.fold_in(_rk, 16), (16,), 18, 1005, jnp.int32)
        itok_B_0_2 = jax.random.randint(jax.random.fold_in(_rk, 17), (16,), 0, 3, jnp.int32)
        return (x, itok_B_0_7, condB_zX, condB_zY, condB_zR, fside_BxSxS_0, itok_B_18_1004, itok_B_0_2)
    x, itok_B_0_7, condB_zX, condB_zY, condB_zR, fside_BxSxS_0, itok_B_18_1004, itok_B_0_2 = _rec_inputs()

    def _L0_cond_setup():
        import jax, jax.numpy as jnp
        import numpy as np
        S, O, H = (8, 256, 256)
        B, N = (32, 128)
        key = jax.random.key(seed)
        k1, k2, k3, k4 = jax.random.split(key, 4)
        x = jax.random.normal(k1, (B, N, H), dtype=jnp.float32)
        subject_id = jax.random.randint(k2, (B,), 0, S)
        wbound = jnp.sqrt(2.0 / 6.0) * jnp.sqrt(3.0 / H)
        weight = jax.random.uniform(k3, (S, O, H), minval=-wbound, maxval=wbound, dtype=jnp.float32)
        bbound = 1.0 / jnp.sqrt(H)
        bias = jax.random.uniform(k4, (S, O), minval=-bbound, maxval=bbound, dtype=jnp.float32)
        return {'x': x, 'subject_id': subject_id, 'weight': weight, 'bias': bias}
    _L0_cond_all = _L0_cond_setup()
    _L0_cond_in = {k: v for k, v in _L0_cond_all.items() if k in ('weight', 'bias')}
    del _L0_cond_all

    def _L1_cond_setup():
        import jax, jax.numpy as jnp
        import numpy as np
        key = jax.random.key(seed)
        k1, k2, k3, k4 = jax.random.split(key, 4)
        B, H, W = (64, 256, 256)
        return {'y': jax.random.uniform(k1, (B, H, W), dtype=jnp.float32), 'zX': jax.random.uniform(k2, (B, 1), dtype=jnp.float32), 'zY': jax.random.uniform(k3, (B, 1), dtype=jnp.float32), 'zR': jax.random.uniform(k4, (B, 1), dtype=jnp.float32), 'dx': 1, 'dy': 1}
    _L1_cond_all = _L1_cond_setup()
    _L1_cond_in = {k: v for k, v in _L1_cond_all.items() if k in ()}
    del _L1_cond_all

    def _L2_cond_setup():
        import jax, jax.numpy as jnp
        import numpy as np
        B, L1, L2, DIN, DOUT, H = (8, 256, 256, 256, 256, 16)
        DH = DOUT // H
        SCALE = 1.0 / np.sqrt(DH).astype(np.float32)
        key = jax.random.key(seed)
        ks = jax.random.split(key, 13)
        s = 0.02
        return {'seq1': jax.random.normal(ks[0], (B, L1, DIN), jnp.float32), 'seq2': jax.random.normal(ks[1], (B, L2, DIN), jnp.float32), 'seq_len1': jax.random.randint(ks[2], (B,), 1, L1 + 1, jnp.int32), 'Wq': jax.random.normal(ks[3], (DIN, DOUT), jnp.float32) * s, 'bq': jnp.zeros((DOUT,), jnp.float32), 'Wk': jax.random.normal(ks[4], (DIN, DOUT), jnp.float32) * s, 'bk': jnp.zeros((DOUT,), jnp.float32), 'Wv': jax.random.normal(ks[5], (DIN, DOUT), jnp.float32) * s, 'bv': jnp.zeros((DOUT,), jnp.float32), 'Wo': jax.random.normal(ks[6], (DOUT, DOUT), jnp.float32) * s, 'bo': jnp.zeros((DOUT,), jnp.float32), 'b_prev': jax.random.normal(ks[7], (1, 1, DIN), jnp.float32) * s, 'b_self': jax.random.normal(ks[8], (1, 1, DIN), jnp.float32) * s}
    _L2_cond_all = _L2_cond_setup()
    _L2_cond_in = {k: v for k, v in _L2_cond_all.items() if k in ('Wq', 'bq', 'Wk', 'bk', 'Wv', 'bv', 'Wo', 'bo', 'b_prev', 'b_self')}
    del _L2_cond_all

    def _L3_cond_setup():
        import jax, jax.numpy as jnp
        import numpy as np
        B, S, D, F, E = (8, 512, 256, 1024, 5)

        def _dense(x, wi_, wo_):
            return jax.nn.relu(x @ wi_) @ wo_
        key = jax.random.key(seed)
        ks = jax.random.split(key, 9)
        sc = 0.02
        return {'hidden_states': jax.random.normal(ks[0], (B, S, D), jnp.float32), 'type_label': jax.random.randint(ks[1], (B,), 0, E, jnp.int32), 'wi': jax.random.normal(ks[2], (E, D, F), jnp.float32) * sc, 'wo': jax.random.normal(ks[3], (E, F, D), jnp.float32) * sc, 'swi': jax.random.normal(ks[4], (2, D, F), jnp.float32) * sc, 'swo': jax.random.normal(ks[5], (2, F, D), jnp.float32) * sc, 'g1': jax.random.normal(ks[6], (3 * D, D), jnp.float32) * sc, 'g2': jax.random.normal(ks[7], (D, 3), jnp.float32) * sc}
    _L3_cond_all = _L3_cond_setup()
    _L3_cond_in = {k: v for k, v in _L3_cond_all.items() if k in ('wi', 'wo', 'swi', 'swo', 'g1', 'g2')}
    del _L3_cond_all
    return {'x': x, 'itok_B_0_7': itok_B_0_7, 'condB_zX': condB_zX, 'condB_zY': condB_zY, 'condB_zR': condB_zR, 'fside_BxSxS_0': fside_BxSxS_0, 'itok_B_18_1004': itok_B_18_1004, 'itok_B_0_2': itok_B_0_2, 'L0_cond_weight': _L0_cond_in['weight'], 'L0_cond_bias': _L0_cond_in['bias'], 'L2_cond_Wq': _L2_cond_in['Wq'], 'L2_cond_bq': _L2_cond_in['bq'], 'L2_cond_Wk': _L2_cond_in['Wk'], 'L2_cond_bk': _L2_cond_in['bk'], 'L2_cond_Wv': _L2_cond_in['Wv'], 'L2_cond_bv': _L2_cond_in['bv'], 'L2_cond_Wo': _L2_cond_in['Wo'], 'L2_cond_bo': _L2_cond_in['bo'], 'L2_cond_b_prev': _L2_cond_in['b_prev'], 'L2_cond_b_self': _L2_cond_in['b_self'], 'L3_cond_wi': _L3_cond_in['wi'], 'L3_cond_wo': _L3_cond_in['wo'], 'L3_cond_swi': _L3_cond_in['swi'], 'L3_cond_swo': _L3_cond_in['swo'], 'L3_cond_g1': _L3_cond_in['g1'], 'L3_cond_g2': _L3_cond_in['g2']}

def reference(x, itok_B_0_7, condB_zX, condB_zY, condB_zR, fside_BxSxS_0, itok_B_18_1004, itok_B_0_2, L0_cond_weight, L0_cond_bias, L2_cond_Wq, L2_cond_bq, L2_cond_Wk, L2_cond_bk, L2_cond_Wv, L2_cond_bv, L2_cond_Wo, L2_cond_bo, L2_cond_b_prev, L2_cond_b_self, L3_cond_wi, L3_cond_wo, L3_cond_swi, L3_cond_swo, L3_cond_g1, L3_cond_g2):
    import jax
    import jax.numpy as jnp

    def _L0_cond_ref(x, subject_id, weight, bias):
        import jax, jax.numpy as jnp
        import numpy as np
        S, O, H = (8, 256, 256)
        B, N = (32, 128)
        W = weight[subject_id]
        b = bias[subject_id]
        y = jnp.einsum('bnh,boh->bno', x, W) + b[:, None, :]
        return y

    def _L1_cond_ref(y, zX, zY, zR, dx, dy):
        import jax, jax.numpy as jnp
        import numpy as np
        yp_x = jnp.pad(y, ((0, 0), (0, 0), (1, 1)), mode='reflect')
        lap_x = (yp_x[:, :, :-2] - 2.0 * y + yp_x[:, :, 2:]) / (dx * dx)
        yp_y = jnp.pad(y, ((0, 0), (1, 1), (0, 0)), mode='reflect')
        lap_y = (yp_y[:, :-2, :] - 2.0 * y + yp_y[:, 2:, :]) / (dy * dy)
        du_dt = zX[:, :, None] * lap_x + zY[:, :, None] * lap_y + zR[:, :, None] * y * (1.0 - y)
        return du_dt

    def _L2_cond_ref(seq1, seq2, seq_len1, Wq, bq, Wk, bk, Wv, bv, Wo, bo, b_prev, b_self):
        import jax, jax.numpy as jnp
        import numpy as np
        B, L1, L2, DIN, DOUT, H = (8, 256, 256, 256, 256, 16)
        DH = DOUT // H
        SCALE = 1.0 / np.sqrt(DH).astype(np.float32)
        b, l1, _ = seq1.shape
        l2 = seq2.shape[1]
        query = seq2 + b_self
        key = jnp.concatenate([seq1 + b_prev, seq2 + b_self], 1)
        value = jnp.concatenate([seq1, seq2], 1)
        q = (query @ Wq + bq).reshape(b, l2, H, DH).transpose(0, 2, 1, 3)
        k = (key @ Wk + bk).reshape(b, l1 + l2, H, DH).transpose(0, 2, 1, 3)
        v = (value @ Wv + bv).reshape(b, l1 + l2, H, DH).transpose(0, 2, 1, 3)
        score_prev = jnp.einsum('bhqd,bhkd->bhqk', q, k[:, :, :l1]) * SCALE
        score_self = (q * k[:, :, l1:]).sum(-1, keepdims=True) * SCALE
        mask = jnp.arange(l1)[None, :] < seq_len1[:, None]
        score_prev = jnp.where(mask[:, None, None, :], score_prev, -jnp.inf)
        score = jnp.concatenate([score_prev, score_self], -1)
        weights = jax.nn.softmax(score, axis=-1)
        attn = jnp.einsum('bhqk,bhkd->bhqd', weights[..., :-1], v[:, :, :l1])
        attn = attn + weights[..., -1:] * v[:, :, l1:]
        attn = attn.transpose(0, 2, 1, 3).reshape(b, l2, H * DH)
        return attn @ Wo + bo

    def _L3_cond_ref(hidden_states, type_label, wi, wo, swi, swo, g1, g2):
        import jax, jax.numpy as jnp
        import numpy as np
        B, S, D, F, E = (8, 512, 256, 1024, 5)

        def _dense(x, wi_, wo_):
            return jax.nn.relu(x @ wi_) @ wo_
        x = hidden_states
        s0 = _dense(x, swi[0], swo[0])
        s1 = _dense(x, swi[1], swo[1])
        wi_sel = wi[type_label]
        wo_sel = wo[type_label]
        h = jax.nn.relu(jnp.einsum('bsd,bdf->bsf', x, wi_sel))
        eo = jnp.einsum('bsf,bfd->bsd', h, wo_sel)
        gate_in = jnp.concatenate([eo[:, 0], s0[:, 0], s1[:, 0]], axis=-1)
        w = jax.nn.softmax(jax.nn.relu(gate_in @ g1) @ g2, axis=-1)
        w = w[:, :, None, None]
        return eo * w[:, 0] + s0 * w[:, 1] + s1 * w[:, 2]
    x = x + _L0_cond_ref(x, itok_B_0_7, L0_cond_weight, L0_cond_bias)
    x = x + _L1_cond_ref(x, condB_zX[:, None], condB_zY[:, None], condB_zR[:, None], 1, 1)
    x = x + _L2_cond_ref(x, fside_BxSxS_0, itok_B_18_1004, L2_cond_Wq, L2_cond_bq, L2_cond_Wk, L2_cond_bk, L2_cond_Wv, L2_cond_bv, L2_cond_Wo, L2_cond_bo, L2_cond_b_prev, L2_cond_b_self)
    x = x + _L3_cond_ref(x, itok_B_0_2, L3_cond_wi, L3_cond_wo, L3_cond_swi, L3_cond_swo, L3_cond_g1, L3_cond_g2)
    return x

_drawn_inputs = setup_inputs


def setup_inputs(seed=0):
    import zlib

    import numpy as np

    out = dict(_drawn_inputs(seed))
    spreads = {'L2_cond_bq': (0.0, 0.8),
     'L2_cond_bk': (0.0, 0.8),
     'L2_cond_bv': (0.0, 0.543),
     'L2_cond_bo': (0.0, 0.1)}
    factors = {'fside_BxSxS_0': 8.0,
     'L2_cond_Wq': 8.0,
     'L2_cond_Wk': 8.0,
     'L2_cond_b_prev': 8.0,
     'L2_cond_b_self': 8.0,
     'L3_cond_g1': 8.0,
     'L3_cond_g2': 8.0}
    for name, (base, spread) in spreads.items():
        noise = np.random.default_rng([zlib.crc32(name.encode()), seed]).standard_normal(out[name].shape)
        drawn = base * np.exp(spread * noise) if base else spread * noise
        out[name] = jnp.asarray(drawn.astype(out[name].dtype))
    for name, factor in factors.items():
        out[name] = (out[name] * factor).astype(out[name].dtype)
    return out
```

```python
from contextlib import ExitStack

import numpy as np

import concourse.bass as bass
from concourse import mybir

ALU = mybir.AluOpType
ACT = mybir.ActivationFunctionType
F32 = mybir.dt.float32
F32R = mybir.dt.float32r
BF16 = mybir.dt.bfloat16
F16 = mybir.dt.float16
I32 = mybir.dt.int32
AX_X = mybir.AxisListType.X

P = 128
B = 16
S = 256
D = 256
C = D // P
H = 16
DH = D // H
SCALE = 1.0 / DH ** 0.5
HALF = H // 2
F = 1024
FC = F // P
NE = 3
CHOSEN = 2
STEPS = 4
LSTEPS = NE * STEPS
VW = 3 * DH + 1
ROWS_MAX = 3 * DH + 1
ROWS_EXP = ROWS_MAX + 2
MASKED = -1.0e30

USES = (["xT", "wT", "sT", "x1", "ks", "q", "lap", "vs", "self", "kp", "vp"]
        + [f"S{h}" for h in range(H)] + ["mT"] + [f"E{h}" for h in range(H)] + ["aT", "wo"])
USE = {name: n for n, name in enumerate(USES)}
NU = len(USES)
assert NU % 2 == 0
ACT_FREES = {"ks"} | {f"E{h}" for h in range(H)}
N_ACT = [sum(x in ACT_FREES for x in USES[:u + 1]) for u in range(NU)]
N_DVE = [u + 1 - N_ACT[u] for u in range(NU)]
HI_OF = {name: n + 1 for n, name in enumerate(["xT", "wT", "sT", "q", "kp", "aT"])}
NHI = len(HI_OF)

FRONT = (["xT", "wT", "sT", "x1", "ks", "q", "lap", "vs", "self", "kp", "vp"]
         + [f"S{h}" for h in range(H)] + ["mT"] + [f"E{h}" for h in range(H)] + ["pvend", "aT", "wo"])
EXPERTS = [f"L{s}" for s in range(LSTEPS)] + ["Lend", "gate", "logits", "mix", "out0", "out1"]
AFTER = {"sT": ["L0"], "q": ["L1"], "vs": ["L2"], "self": ["L3"], "vp": ["L4"], "S5": ["L5"],
         "S10": ["L6"], "S15": ["L7"], "mT": ["L8", "L9"], "E1": ["L10"], "E3": ["L11"],
         "E5": ["Lend"], "E7": ["gate"], "E10": ["logits"], "E12": ["mix"], "E15": ["out0", "out1"]}
BOTH = [x for stage in FRONT for x in [stage] + AFTER.get(stage, [])]
assert [x for x in BOTH if x in EXPERTS] == EXPERTS

BQ, BK, BO, B_PREV, B_SELF, NVEC = range(6)
FRONT_LINKS = 11
EXPERT_LINKS = 6


def wait(eng, sem, per_turn, turn, n):
    value = turn * per_turn + n
    if isinstance(value, int) and value <= 0:
        return
    eng.wait_ge(sem, value)


def build(nc, x, side, seq_len, subject, label, z, w0, b0, wqkvo, vecs, bv, wi, wo, swi, swo,
          g1, g2, consts, iota, out):
    with ExitStack() as ctx:
        def sb(name, shape, dt=F32):
            return ctx.enter_context(nc.sbuf_tensor(name, shape, dt))

        def bank(name):
            return ctx.enter_context(nc.psum_tensor(name, [P, 512], F32))

        def sem(name):
            return ctx.enter_context(nc.semaphore(name))

        exp_hi = sb("exp_hi", [P, NE, 2 * C * F], F32R)
        exp_lo = sb("exp_lo", [P, NE, 2 * C * F], F32R)
        raw = sb("raw", [P, C * F])
        lin_hi = sb("lin_hi", [P, 4, C * D], F32R)
        lin_lo = sb("lin_lo", [P, 4, C * D], F32R)
        gate1 = sb("gate1", [P, NE * C, D])
        gate2 = sb("gate2", [P, C, 3])
        ident = sb("ident", [P, P])
        head_ones = sb("head_ones", [P, C * H])
        lap_mats = sb("lap_mats", [P, 4 * P], F32R)
        vec = sb("vec", [P, C, NVEC])
        bv_row = sb("bv_row", [P, D])
        ebias = sb("ebias", [P, 3, C])
        iota_sb = sb("iota_sb", [B, S])
        len_sb = sb("len_sb", [B, 1], I32)
        len_f = sb("len_f", [B, 1])
        mask_rows = sb("mask_rows", [B, S], F32R)
        subject_sb = sb("subject_sb", [1, B], I32)
        label_sb = sb("label_sb", [1, B], I32)

        x_nat = sb("x_nat", [P, C, D])
        s_nat = sb("s_nat", [P, C, D])
        w0_nat = sb("w0_nat", [P, C, D])
        b0_sb = sb("b0_sb", [P, C])
        z_sb = sb("z_sb", [P, 3])
        z_neg = sb("z_neg", [P, 1])
        z_one = sb("z_one", [P, 1])
        x1T = sb("x1T", [P, C, S])
        att = x1T
        x_hi = sb("x_hi", [P, C, S], F32R)
        x_lo = sb("x_lo", [P, C, S], F32R)
        s_hi = sb("s_hi", [P, C, S], F32R)
        s_lo = sb("s_lo", [P, C, S], F32R)
        p_hi = sb("p_hi", [P, C, S], F32R)
        p_lo = sb("p_lo", [P, C, S], F32R)
        ksT = sb("ksT", [P, C, S])
        lapy = sb("lapy", [P, C, S])
        v_prev = lapy
        react = sb("react", [P, C, S])
        v_rest = react
        x2T = sb("x2T", [P, C, S])
        x3T = sb("x3T", [P, C, S])
        x3_hi = sb("x3_hi", [P, C, S], F32R)
        x3_lo = sb("x3_lo", [P, C, S], F32R)
        q_rows = sb("q_rows", [P, HALF, S], F32R)
        k_rows = sb("k_rows", [P, HALF, S], F32R)
        v_self = sb("v_self", [P, C, D])
        v_cols = sb("v_cols", [P, C, H, VW], BF16)
        s_self = sb("s_self", [P, C, H])
        s_max = sb("s_max", [P, C, H])
        d_self = sb("d_self", [P, C, H])
        p_self = sb("p_self", [P, C, H])
        max_rows = sb("max_rows", [H, 2, S], F32R)
        prob = sb("prob", [P, 2, 2 * S])
        prob_hi = sb("prob_hi", [P, 2, 2 * S], F16)
        prob_lo = sb("prob_lo", [P, 2, 2 * S], F16)
        den = sb("den", [P, C, H])

        hid_hi = sb("hid_hi", [P, 2, 2 * S], F32R)
        hid_lo = sb("hid_lo", [P, 2, 2 * S], F32R)
        e_out = sb("e_out", [P, NE, C, S])
        gate_h = sb("gate_h", [P, C, P])
        gate_s = sb("gate_s", [P, 12])
        out_nat = sb("out_nat", [P, C, D])

        mask_dram = nc.dram_tensor("mask_scratch", (B, S), F32R, kind="Internal").ap()

        front_bank = [bank("front0"), bank("front1")]
        pv_bank = [bank("pv0"), bank("pv1")]
        hid_bank = [bank("hid0"), bank("hid1")]
        out_bank = [bank("out0"), bank("out1")]

        consts_in = sem("consts_in")
        lin_in = sem("lin_in")
        consts_set = sem("consts_set")
        bias_done = sem("bias_done")
        mask_set = sem("mask_set")
        rows_set = sem("rows_set")
        lin_split = sem("lin_split")
        x_in = sem("x_in")
        s_in = sem("s_in")
        w0_in = sem("w0_in")
        small_in = sem("small_in")
        raw_in = sem("raw_in")
        filled = sem("filled")
        freed_act = sem("freed_act")
        freed_dve = sem("freed_dve")
        hi_done = sem("hi_done")
        x1_split = sem("x1_split")
        x2_split = sem("x2_split")
        x3_split = sem("x3_split")
        q_placed = sem("q_placed")
        k_placed = sem("k_placed")
        max_placed = sem("max_placed")
        v_hi = sem("v_hi")
        v_link = sem("v_link")
        v_split = sem("v_split")
        max_done = sem("max_done")
        d_self_done = sem("d_self_done")
        p_self_done = sem("p_self_done")
        prob_split = sem("prob_split")
        pv_done = sem("pv_done")
        pv_freed = sem("pv_freed")
        att_done = sem("att_done")
        front_link = sem("front_link")
        w_hi_done = sem("w_hi_done")
        w_split = sem("w_split")
        chosen_hi = sem("chosen_hi")
        hid_filled = sem("hid_filled")
        hid_hi_done = sem("hid_hi_done")
        hid_split = sem("hid_split")
        step_done = sem("step_done")
        e_out_done = sem("e_out_done")
        gate_done = sem("gate_done")
        gate_relu = sem("gate_relu")
        logits_done = sem("logits_done")
        logits_read = sem("logits_read")
        gate_exp = sem("gate_exp")
        mixed = sem("mixed")
        out_copied = sem("out_copied")
        stored = sem("stored")
        expert_link = sem("expert_link")

        def front_psum(name):
            return front_bank[USE[name] % 2]

        def chunked(t):
            return t[:, :].rearrange("p (c t) -> p c t", c=C)

        def wait_filled(eng, i, name):
            wait(eng, filled, NU, i, USE[name] + 1)

        def wait_freed_dve(eng, i, name):
            wait(eng, freed_dve, N_DVE[-1], i, N_DVE[USE[name]])

        def wait_freed_act(eng, i, name):
            wait(eng, freed_act, N_ACT[-1], i, N_ACT[USE[name]])

        def expert_w(part, e):
            w_in = part[:, e, 0:C * F].rearrange("p (k f) -> p k f", k=C)
            w_out = part[:, e, C * F:2 * C * F].rearrange("p (f d) -> p f d", d=D)
            return w_in, w_out

        block = ctx.enter_context(nc.Block())

        @block.sync
        def _(sp):
            def load_x(b):
                sp.dma_start(x_nat[:, :, :], x[bass.ds(b, 1)].rearrange("o (n p) d -> p (o n) d", p=P)).then_inc(x_in, 16)

            def load_s(b):
                sp.dma_start(s_nat[:, :, :], side[bass.ds(b, 1)].rearrange("o (n p) d -> p (o n) d", p=P)).then_inc(s_in, 16)

            def chooser(row, b, count):
                return sp.value_load(row[0:1, bass.ds(b, 1)], min_val=0, max_val=count - 1)

            def load_w0(who):
                sp.dma_start(w0_nat[:, :, :], w0[bass.ds(who, 1)].rearrange("o (n p) h -> p (o n) h", p=P)).then_inc(w0_in, 16)

            def load_small(b, who):
                sp.dma_start(b0_sb[:, :], b0[bass.ds(who, 1)].rearrange("o p c -> (o p) c")).then_inc(small_in, 16)
                sp.dma_start(z_sb[:, :], z[bass.ds(b, 1)].to_broadcast([P, 3])).then_inc(small_in, 16)

            def load_wi(kind):
                sp.dma_start(raw[:, :].rearrange("p (k f) -> p k f", k=C),
                             wi[bass.ds(kind, 1)].rearrange("o (k p) f -> p (o k) f", p=P)).then_inc(raw_in, 16)

            def load_wo(kind):
                sp.dma_start(raw[:, :].rearrange("p (f d) -> p f d", d=D),
                             wo[bass.ds(kind, 1)].rearrange("o (f p) d -> p (o f) d", p=P)).then_inc(raw_in, 16)

            def load_shared(n):
                if n % 2 == 0:
                    sp.dma_start(raw[:, :].rearrange("p (k f) -> p k f", k=C),
                                 swi[n // 2].rearrange("(k p) f -> p k f", p=P)).then_inc(raw_in, 16)
                else:
                    sp.dma_start(raw[:, :].rearrange("p (f d) -> p f d", d=D),
                                 swo[n // 2].rearrange("(f p) d -> p f d", p=P)).then_inc(raw_in, 16)

            def place(rows, part, first_row, done):
                for c in range(C):
                    for e in range(2):
                        sp.dma_start(rows[64 * e + first_row:64 * e + first_row + DH, 4 * c:4 * c + 4, :].bitcast(F32),
                                     part[64 * e:64 * e + 64, c, :].bitcast(F32)).then_inc(done, 16)

            def stage(name, i, first):
                nxt = (i + 1) % B
                if name == "xT":
                    wait_filled(sp, i, "xT")
                    load_x(nxt)
                elif name == "wT":
                    who = chooser(subject_sb, nxt, w0.shape[0])
                    wait_filled(sp, i, "wT")
                    load_w0(who)
                elif name == "sT":
                    wait_filled(sp, i, "sT")
                    load_s(nxt)
                    if first:
                        sp.wait_ge(w_split, 1)
                        load_shared(1)
                elif name == "q":
                    wait_freed_dve(sp, i, "q")
                    if first:
                        sp.wait_ge(rows_set, 2)
                    place(q_rows, p_hi, 0, q_placed)
                    place(q_rows, p_lo, DH, q_placed)
                    place(q_rows, p_hi, 2 * DH, q_placed)
                    if first:
                        sp.wait_ge(w_split, 2)
                        load_shared(2)
                    else:
                        kind = chooser(label_sb, i - 1, wo.shape[0])
                        wait(sp, w_split, 2, i - 1, 5)
                        load_wo(kind)
                elif name == "kp":
                    who = chooser(subject_sb, nxt, w0.shape[0])
                    wait(sp, x2_split, 1, i, 1)
                    load_small(nxt, who)
                    wait_freed_dve(sp, i, "kp")
                    place(k_rows, p_hi, 0, k_placed)
                    place(k_rows, p_hi, DH, k_placed)
                    place(k_rows, p_lo, 2 * DH, k_placed)
                    for e in range(2):
                        sp.dma_start(k_rows[64 * e + 3 * DH:64 * e + 3 * DH + 1, :, :].bitcast(F32),
                                     mask_dram[bass.ds(i, 1), :].bitcast(F32).unsqueeze(1).to_broadcast([1, HALF, S])
                                     ).then_inc(k_placed, 16)
                elif name == "vp" and first:
                    sp.wait_ge(w_split, 3)
                    load_shared(3)
                elif name == "mT":
                    wait_freed_dve(sp, i, "mT")
                    for e in range(2):
                        for j in range(2):
                            row = 64 * e + ROWS_MAX + j
                            sp.dma_start(q_rows[row:row + 1, :, :].bitcast(F32),
                                         max_rows[HALF * e:HALF * e + HALF, j, :].bitcast(F32)).then_inc(max_placed, 16)
                elif name == "E2":
                    kind = chooser(label_sb, i, wi.shape[0])
                    wait(sp, w_split, 2, i, 4)
                    load_wi(kind)

            def store(j):
                wait(sp, out_copied, C, j, C)
                sp.dma_start(out[bass.ds(j, 1)].rearrange("o (n p) d -> p (o n) d", p=P), out_nat[:, :, :]).then_inc(stored, 16)

            sp.dma_start(subject_sb[:, :], subject).then_inc(consts_in, 16)
            sp.dma_start(label_sb[:, :], label).then_inc(consts_in, 16)
            sp.dma_start(ident[:, :], consts[:, 0:P]).then_inc(consts_in, 16)
            load_x(0)
            sp.wait_ge(consts_in, 48)
            load_w0(chooser(subject_sb, 0, w0.shape[0]))
            load_s(0)
            load_small(0, chooser(subject_sb, 0, w0.shape[0]))
            for n in range(4):
                sp.dma_start(raw[:, n * C * D:(n + 1) * C * D].rearrange("p (k f) -> p k f", k=C),
                             wqkvo[n].rearrange("(k p) f -> p k f", p=P)).then_inc(lin_in, 16)
            sp.dma_start(vec[:, :, :], vecs).then_inc(consts_in, 16)
            sp.dma_start(e_out[:, 0, :, :].rearrange("p c t -> p (c t)"), consts[:, P:5 * P]).then_inc(consts_in, 16)
            sp.dma_start(head_ones[:, :], consts[:, 5 * P:5 * P + C * H]).then_inc(consts_in, 16)
            sp.dma_start(iota_sb[:, :], iota).then_inc(consts_in, 16)
            sp.dma_start(len_sb[:, :], seq_len).then_inc(consts_in, 16)
            sp.dma_start(bv_row[:, :], bv.to_broadcast([P, D])).then_inc(consts_in, 16)
            sp.dma_start(gate1[:, :, :], g1.rearrange("(k p) f -> p k f", p=P)).then_inc(consts_in, 16)
            sp.dma_start(gate2[:, :, :], g2.rearrange("(k p) f -> p k f", p=P)).then_inc(consts_in, 16)
            sp.wait_ge(mask_set, 1)
            sp.dma_start(mask_dram.bitcast(F32), mask_rows[:, :].bitcast(F32)).then_inc(stored, 16)
            sp.wait_ge(stored, 16)
            sp.wait_ge(lin_split, 1)
            sp.wait_ge(bias_done, 1)
            load_shared(0)
            for name in FRONT:
                stage(name, 0, True)
            with sp.Fori(1, B) as i:
                for name in BOTH:
                    if name == "out1":
                        store(i - 1)
                    else:
                        stage(name, i, False)
            kind = chooser(label_sb, B - 1, wo.shape[0])
            wait(sp, w_split, 2, B - 1, 5)
            load_wo(kind)
            store(B - 1)
            sp.wait_ge(x_in, 16 * (B + 1))
            sp.wait_ge(s_in, 16 * (B + 1))
            sp.wait_ge(w0_in, 16 * (B + 1))
            sp.wait_ge(small_in, 32 * (B + 1))
            sp.wait_ge(stored, 16 * (B + 1))

        @block.tensor
        def _(pe):
            def product(acc, w_hi, w_lo, a_hi, a_lo, first, last):
                nc.tensor.matmul(acc, w_hi, a_hi, start=first, stop=False)
                nc.tensor.matmul(acc, w_hi, a_lo, start=False, stop=False)
                return nc.tensor.matmul(acc, w_lo, a_hi, start=False, stop=last)

            def linear(n):
                return (lin_hi[:, n, :].rearrange("p (k f) -> p k f", k=C),
                        lin_lo[:, n, :].rearrange("p (k f) -> p k f", k=C))

            def feature_major(psum, w, a_hi, a_lo):
                for c in range(C):
                    for k in range(C):
                        last = product(psum[:, c * S:(c + 1) * S], w[0][:, k, c * P:(c + 1) * P],
                                       w[1][:, k, c * P:(c + 1) * P], a_hi[:, k, :], a_lo[:, k, :], k == 0, k == C - 1)
                return last

            def token_major(psum, w, a_hi, a_lo):
                for t in range(C):
                    for k in range(C):
                        last = product(psum[:, t * D:(t + 1) * D], a_hi[:, k, t * P:(t + 1) * P],
                                       a_lo[:, k, t * P:(t + 1) * P], w[0][:, k, :], w[1][:, k, :], k == 0, k == C - 1)
                return last

            def transposed(psum, src):
                for c in range(C):
                    for t in range(C):
                        last = nc.tensor.transpose(psum[:, c * S + t * P:c * S + (t + 1) * P],
                                                   src[:, t, c * P:(c + 1) * P], ident[:, :])
                return last

            def open_bank(i, name):
                u, turn = USE[name] - 2, i
                if u < 0:
                    u, turn = u + NU, i - 1
                (wait_freed_act if USES[u] in ACT_FREES else wait_freed_dve)(pe, turn, USES[u])
                return front_bank[USE[name] % 2]

            def attend(i, h):
                wait(pe, prob_split, H, i, h + 1)
                if h == 0:
                    wait(pe, v_split, 1, i, 1)
                    wait(pe, pv_freed, 2, i - 1, 2)
                if h == HALF:
                    wait(pe, pv_freed, 2, i, 1)
                for t in range(C):
                    acc = pv_bank[t][:, (h % HALF) * VW:(h % HALF + 1) * VW]
                    for k in range(C):
                        at = k * S + t * P
                        nc.tensor.matmul(acc, prob_hi[:, h % 2, at:at + P], v_cols[:, k, h, :], start=(k == 0), stop=False)
                        last = nc.tensor.matmul(acc, prob_lo[:, h % 2, at:at + P], v_cols[:, k, h, :],
                                                start=False, stop=(k == C - 1))
                last.then_inc(pv_done, 1)

            def front(name, i):
                if name == "pvend":
                    attend(i, H - 1)
                    return
                psum = open_bank(i, name)
                if name == "xT":
                    wait(pe, x_in, 16, i, 16)
                    last = transposed(psum, x_nat)
                elif name == "wT":
                    wait(pe, w0_in, 16, i, 16)
                    last = transposed(psum, w0_nat)
                elif name == "sT":
                    wait(pe, s_in, 16, i, 16)
                    last = transposed(psum, s_nat)
                elif name == "x1":
                    wait_freed_dve(pe, i, "wT")
                    last = feature_major(psum, (p_hi, p_lo), x_hi, x_lo)
                elif name == "ks":
                    wait_freed_dve(pe, i, "sT")
                    last = feature_major(psum, linear(1), s_hi, s_lo)
                elif name == "q":
                    last = feature_major(psum, linear(0), s_hi, s_lo)
                elif name == "lap":
                    wait(pe, x1_split, 1, i, 1)
                    for c in range(C):
                        acc = psum[:, c * S:(c + 1) * S]
                        own = lap_mats[:, c * P:(c + 1) * P]
                        across = lap_mats[:, (2 + c) * P:(3 + c) * P]
                        nc.tensor.matmul(acc, own, x_hi[:, c, :], start=True, stop=False)
                        nc.tensor.matmul(acc, own, x_lo[:, c, :], start=False, stop=False)
                        nc.tensor.matmul(acc, across, x_hi[:, 1 - c, :], start=False, stop=False)
                        last = nc.tensor.matmul(acc, across, x_lo[:, 1 - c, :], start=False, stop=True)
                elif name == "vs":
                    last = token_major(psum, linear(2), s_hi, s_lo)
                elif name == "self":
                    wait_freed_dve(pe, i, "q")
                    for t in range(C):
                        for c in range(C):
                            last = nc.tensor.matmul(psum[:, t * H:(t + 1) * H], ksT[:, c, t * P:(t + 1) * P],
                                                    head_ones[:, c * H:(c + 1) * H], start=(c == 0), stop=(c == C - 1))
                elif name == "kp":
                    wait(pe, x2_split, 1, i, 1)
                    last = feature_major(psum, linear(1), x_hi, x_lo)
                elif name == "vp":
                    last = token_major(psum, linear(2), x_hi, x_lo)
                elif name[0] == "S":
                    h = int(name[1:])
                    if h == 0:
                        wait(pe, q_placed, 16 * 12, i, 16 * 12)
                        wait(pe, k_placed, 16 * 14, i, 16 * 14)
                    at, slot = 64 * (h // HALF), h % HALF
                    for t in range(C):
                        last = nc.tensor.matmul(psum[:, t * S:(t + 1) * S], q_rows[at:at + ROWS_MAX, slot, t * P:(t + 1) * P],
                                                k_rows[at:at + ROWS_MAX, slot, :], start=True, stop=True)
                elif name == "mT":
                    wait(pe, max_done, 1, i, 1)
                    for t in range(C):
                        last = nc.tensor.transpose(psum[0:H, t * P:(t + 1) * P], s_max[:, t, :], ident[:, :])
                elif name[0] == "E":
                    h = int(name[1:])
                    if h == 0:
                        wait(pe, max_placed, 16 * 4, i, 16 * 4)
                    at, slot = 64 * (h // HALF), h % HALF
                    for k in range(C):
                        last = nc.tensor.matmul(psum[:, k * S:(k + 1) * S], k_rows[at:at + ROWS_EXP, slot, k * P:(k + 1) * P],
                                                q_rows[at:at + ROWS_EXP, slot, :], start=True, stop=True)
                elif name == "aT":
                    wait(pe, att_done, 1, i, 1)
                    last = transposed(psum, att)
                elif name == "wo":
                    wait_freed_dve(pe, i, "aT")
                    last = feature_major(psum, linear(3), s_hi, s_lo)
                last.then_inc(filled, 1)
                if name[0] == "E" and name != "E0":
                    attend(i, int(name[1:]) - 1)

            def hidden(s, j):
                e = s // STEPS
                (hi, _), (lo, _) = expert_w(exp_hi, e), expert_w(exp_lo, e)
                if s == 0:
                    wait(pe, x3_split, 1, j, 1)
                    pe.wait_ge(w_split, 4)
                if s == CHOSEN * STEPS:
                    wait(pe, w_split, 2, j, 5)
                if s >= 2:
                    wait(pe, hid_split, LSTEPS, j, s - 1)
                psum = hid_bank[s % 2]
                for f in range(2):
                    at = (2 * (s % STEPS) + f) * P
                    for k in range(C):
                        last = product(psum[:, f * S:(f + 1) * S], hi[:, k, at:at + P], lo[:, k, at:at + P],
                                       x3_hi[:, k, :], x3_lo[:, k, :], k == 0, k == C - 1)
                last.then_inc(hid_filled, 1)

            def project(s, j):
                e = s // STEPS
                (_, hi), (_, lo) = expert_w(exp_hi, e), expert_w(exp_lo, e)
                wait(pe, hid_split, LSTEPS, j, s + 1)
                if s and s % STEPS == 0:
                    wait(pe, e_out_done, NE, j, e)
                if s == CHOSEN * STEPS:
                    wait(pe, w_split, 2, j, 6)
                for f in range(2):
                    n = 2 * (s % STEPS) + f
                    for c in range(C):
                        last = product(out_bank[c][:, 0:S], hi[:, n, c * P:(c + 1) * P], lo[:, n, c * P:(c + 1) * P],
                                       hid_hi[:, s % 2, f * S:(f + 1) * S], hid_lo[:, s % 2, f * S:(f + 1) * S],
                                       n == 0, n == FC - 1)
                last.then_inc(step_done, 1)

            def experts(name, j):
                if name[1:].isdigit() and name[0] == "L":
                    s = int(name[1:])
                    hidden(s, j)
                    if s:
                        project(s - 1, j)
                elif name == "Lend":
                    project(LSTEPS - 1, j)
                elif name == "gate":
                    wait(pe, e_out_done, NE, j, NE)
                    for c in range(C):
                        for n in range(NE * C):
                            e = (CHOSEN, 0, 1)[n // C]
                            last = nc.tensor.matmul(out_bank[0][:, c:c + 1], gate1[:, n, c * P:(c + 1) * P],
                                                    e_out[:, e, n % C, 0:1], start=(n == 0), stop=(n == NE * C - 1))
                    last.then_inc(gate_done, 1)
                elif name == "logits":
                    wait(pe, gate_relu, 1, j, 1)
                    for c in range(C):
                        last = nc.tensor.matmul(out_bank[1][:, 0:3], gate_h[:, c, :], gate2[:, c, :],
                                                start=(c == 0), stop=(c == C - 1))
                    last.then_inc(logits_done, 1)
                elif name in ("out0", "out1"):
                    t = int(name[3])
                    if t == 0:
                        wait(pe, mixed, 1, j, 1)
                    wait(pe, hid_split, LSTEPS, j, LSTEPS - 1 + t)
                    for c in range(C):
                        last = nc.tensor.transpose(hid_bank[t][:, c * P:(c + 1) * P],
                                                   e_out[:, CHOSEN, c, t * P:(t + 1) * P], ident[:, :])
                    last.then_inc(hid_filled, 1)

            pe.wait_ge(lin_in, 64)
            pe.wait_ge(consts_in, 16 * 11)
            for c in range(C):
                for k in range(C):
                    at = k * D + c * P
                    nc.tensor.matmul(pv_bank[0][:, c:c + 1], raw[:, at:at + P], vec[:, k, B_SELF:B_SELF + 1],
                                     start=(k == 0), stop=(k == C - 1))
            for c in range(C):
                for k in range(C):
                    at = C * D + k * D + c * P
                    last = nc.tensor.matmul(pv_bank[0][:, 2 + 2 * c:4 + 2 * c], raw[:, at:at + P],
                                            vec[:, k, B_PREV:B_PREV + 2], start=(k == 0), stop=(k == C - 1))
            last.then_inc(bias_done, 1)
            pe.wait_ge(consts_set, 4)
            pe.wait_ge(lin_split, 1)
            for name in FRONT:
                front(name, 0)
            with pe.Fori(1, B) as i:
                for name in BOTH:
                    if name in EXPERTS:
                        experts(name, i - 1)
                    else:
                        front(name, i)
            for name in EXPERTS:
                experts(name, B - 1)

        @block.scalar
        def _(act):
            def round_hi(i, name, dst, bias=None):
                wait_filled(act, i, name)
                psum = chunked(front_psum(name))
                if bias is None:
                    last = nc.scalar.activation(dst[:, :, :], psum, ACT.Copy)
                else:
                    for c in range(C):
                        last = nc.scalar.activation(dst[:, c, :], psum[:, c, :], ACT.Identity, bias=bias[:, c:c + 1])
                last.then_inc(hi_done, 1)

            def front(name, i):
                if name == "xT":
                    wait_filled(act, i, name)
                    nc.scalar.activation(x1T[:, :, :], chunked(front_psum(name)), ACT.Copy)
                    round_hi(i, name, x_hi)
                elif name == "wT":
                    wait(act, k_placed, 16 * 14, i - 1, 16 * 14)
                    round_hi(i, name, p_hi)
                elif name == "sT":
                    round_hi(i, name, s_hi)
                elif name == "ks":
                    wait_filled(act, i, name)
                    psum = chunked(front_psum(name))
                    for c in range(C):
                        last = nc.scalar.activation(ksT[:, c, :], psum[:, c, :], ACT.Identity, bias=ebias[:, 1, c:c + 1])
                    last.then_inc(freed_act, 1)
                elif name == "q":
                    round_hi(i, name, p_hi, ebias[:, 0, :])
                elif name == "kp":
                    wait(act, q_placed, 16 * 12, i, 16 * 12)
                    round_hi(i, name, p_hi, ebias[:, 2, :])
                elif name == "vp":
                    wait_freed_dve(act, i, "vp")
                    wait(act, pv_done, H, i - 1, H)
                    for t in range(C):
                        last = nc.scalar.activation(v_cols[:, t, :, 0:DH], v_prev[:, t, :].rearrange("p (h d) -> p h d", d=DH), ACT.Copy)
                    last.then_inc(v_hi, 1)
                elif name == "mT":
                    wait(act, d_self_done, 1, i, 1)
                    nc.scalar.activation(p_self[:, :, :], d_self[:, :, :], ACT.Exp, scale=SCALE).then_inc(p_self_done, 1)
                elif name[0] == "E":
                    h = int(name[1:])
                    wait_filled(act, i, name)
                    wait(act, prob_split, H, i, h - 1)
                    psum = front_psum(name)
                    nc.scalar.activation(prob[:, h % 2, :], psum[:, :], ACT.Exp, scale=SCALE)
                    wait(act, pv_done, H, i, h - 1)
                    nc.scalar.activation(prob_hi[:, h % 2, :], psum[:, :], ACT.Exp, scale=SCALE).then_inc(freed_act, 1)
                elif name == "aT":
                    round_hi(i, name, s_hi)

            def chosen_hi_part(n, j):
                wait(act, raw_in, 32, j, 16 * (4 + n + 1))
                nc.scalar.activation(exp_hi[:, CHOSEN, n * C * F:(n + 1) * C * F], raw[:, :], ACT.Copy).then_inc(chosen_hi, 1)

            def keep_output(e, j):
                wait(act, step_done, LSTEPS, j, (e + 1) * STEPS)
                for c in range(C):
                    last = nc.scalar.activation(e_out[:, e, c, :], out_bank[c][:, 0:S], ACT.Copy)
                last.then_inc(e_out_done, 1)

            def experts(name, j):
                if name[1:].isdigit() and name[0] == "L":
                    s = int(name[1:])
                    wait(act, hid_filled, LSTEPS + C, j, s + 1)
                    if s >= 2:
                        wait(act, step_done, LSTEPS, j, s - 1)
                    nc.scalar.activation(hid_hi[:, s % 2, :], hid_bank[s % 2][:, :], ACT.Relu).then_inc(hid_hi_done, 1)
                    if s and s % STEPS == 0:
                        keep_output(s // STEPS - 1, j)
                elif name == "Lend":
                    keep_output(NE - 1, j)
                elif name == "logits":
                    wait(act, logits_read, 1, j, 1)
                    nc.scalar.activation(gate_s[:, 4:7], gate_s[:, 1:4], ACT.Exp).then_inc(gate_exp, 1)
                elif name in ("out0", "out1"):
                    t = int(name[3])
                    wait(act, hid_filled, LSTEPS + C, j, LSTEPS + t + 1)
                    if t == 0:
                        wait(act, stored, 16, j, 16)
                    nc.scalar.activation(out_nat[:, t, :], hid_bank[t][:, 0:D], ACT.Copy).then_inc(out_copied, 1)

            act.wait_ge(consts_set, 4)
            act.wait_ge(rows_set, 3)
            for name in FRONT:
                front(name, 0)
            with act.Fori(1, B) as i:
                for name in BOTH:
                    if name in EXPERTS:
                        experts(name, i - 1)
                    else:
                        front(name, i)
                    if name == "xT":
                        chosen_hi_part(0, i - 1)
                    elif name == "vs":
                        chosen_hi_part(1, i - 1)
            chosen_hi_part(0, B - 1)
            for name in EXPERTS:
                experts(name, B - 1)
                if name == "L4":
                    chosen_hi_part(1, B - 1)

        @block.vector
        def _(dve):
            linked = {}

            def link(ins, sem_, per_turn, turn):
                linked[sem_] = linked.get(sem_, 0) + 1
                ins.then_inc(sem_, 1)
                wait(dve, sem_, per_turn, turn, linked[sem_])

            def lo_part(i, name, hi, lo, bias=None):
                wait(dve, hi_done, NHI, i, HI_OF[name])
                psum = chunked(front_psum(name))
                if bias is None:
                    return nc.vector.tensor_tensor(lo[:, :, :], psum, hi[:, :, :].bitcast(F32), ALU.subtract)
                for c in range(C):
                    last = nc.vector.scalar_tensor_tensor(lo[:, c, :], psum[:, c, :], bias[:, c:c + 1],
                                                          hi[:, c, :].bitcast(F32), ALU.add, ALU.subtract)
                return last

            def front(name, i):
                def linkf(ins):
                    link(ins, front_link, FRONT_LINKS, i)

                def split(src, hi, lo):
                    linkf(nc.vector.tensor_copy(hi[:, :, :], src[:, :, :]))
                    return nc.vector.tensor_tensor(lo[:, :, :], src[:, :, :], hi[:, :, :].bitcast(F32), ALU.subtract)

                psum = chunked(front_psum(name)) if name in USE else None
                if name == "xT":
                    lo_part(i, name, x_hi, x_lo).then_inc(freed_dve, 1)
                elif name == "wT":
                    lo_part(i, name, p_hi, p_lo).then_inc(freed_dve, 1)
                elif name == "sT":
                    lo_part(i, name, s_hi, s_lo).then_inc(freed_dve, 1)
                elif name == "x1":
                    wait_filled(dve, i, name)
                    wait(dve, small_in, 32, i, 32)
                    nc.vector.tensor_scalar(z_neg[:, :], z_sb[:, 2:3], -1.0, None, ALU.mult)
                    nc.vector.tensor_scalar(z_one[:, :], z_sb[:, 2:3], 1.0, None, ALU.add)
                    nc.vector.scalar_tensor_tensor(x1T[:, 0, :], psum[:, 0, :], b0_sb[:, 0:1], x1T[:, 0, :], ALU.add, ALU.add)
                    nc.vector.scalar_tensor_tensor(x1T[:, 1, :], psum[:, 1, :], b0_sb[:, 1:2], x1T[:, 1, :],
                                                   ALU.add, ALU.add).then_inc(freed_dve, 1)
                    wait_freed_dve(dve, i, name)
                    split(x1T, x_hi, x_lo).then_inc(x1_split, 1)
                    nc.vector.tensor_tensor(lapy[:, :, 1:S - 1], x1T[:, :, 0:S - 2], x1T[:, :, 2:S], ALU.add)
                    linkf(nc.vector.tensor_scalar(lapy[:, :, 0:S:S - 1], x1T[:, :, 1:S - 1:S - 3], 2.0, None, ALU.mult))
                    linkf(nc.vector.scalar_tensor_tensor(lapy[:, :, :], x1T[:, :, :], -2.0, lapy[:, :, :], ALU.mult, ALU.add))
                    linkf(nc.vector.tensor_scalar(react[:, :, :], x1T[:, :, :], z_neg[:, :], z_one[:, :], ALU.mult, ALU.add))
                    linkf(nc.vector.tensor_tensor(react[:, :, :], react[:, :, :], x1T[:, :, :], ALU.mult))
                    linkf(nc.vector.scalar_tensor_tensor(react[:, :, :], lapy[:, :, :], z_sb[:, 1:2], react[:, :, :],
                                                         ALU.mult, ALU.add))
                elif name == "q":
                    lo_part(i, name, p_hi, p_lo, ebias[:, 0, :])
                    wait_freed_act(dve, i, "ks")
                    for c in range(C):
                        last = nc.vector.scalar_tensor_tensor(ksT[:, c, :], psum[:, c, :], ebias[:, 0, c:c + 1],
                                                              ksT[:, c, :], ALU.add, ALU.mult)
                    last.then_inc(freed_dve, 1)
                elif name == "lap":
                    wait_filled(dve, i, name)
                    nc.vector.scalar_tensor_tensor(x2T[:, :, :], psum, z_sb[:, 0:1], react[:, :, :],
                                                   ALU.mult, ALU.add).then_inc(freed_dve, 1)
                    wait_freed_dve(dve, i, name)
                    split(x2T, x_hi, x_lo).then_inc(x2_split, 1)
                elif name == "vs":
                    wait_filled(dve, i, name)
                    for t in range(C):
                        last = nc.vector.tensor_tensor(v_self[:, t, :], psum[:, t, :], bv_row[:, :], ALU.add)
                    last.then_inc(freed_dve, 1)
                elif name == "self":
                    wait_filled(dve, i, name)
                    nc.vector.tensor_copy(s_self[:, :, :], front_psum(name)[:, 0:C * H].rearrange("p (t h) -> p t h", h=H)
                                          ).then_inc(freed_dve, 1)
                elif name == "kp":
                    lo_part(i, name, p_hi, p_lo, ebias[:, 2, :]).then_inc(freed_dve, 1)
                elif name == "vp":
                    wait_filled(dve, i, name)
                    for t in range(C):
                        last = nc.vector.tensor_tensor(v_prev[:, t, :], psum[:, t, :], bv_row[:, :], ALU.add)
                    last.then_inc(freed_dve, 1)
                elif name[0] == "S":
                    h = int(name[1:])
                    wait_filled(dve, i, name)
                    nc.vector.tensor_reduce(s_max[:, :, h:h + 1], psum, AX_X, ALU.max).then_inc(freed_dve, 1)
                    if h == H - 1:
                        wait_freed_dve(dve, i, name)
                        nc.vector.tensor_tensor(s_max[:, :, :], s_max[:, :, :], s_self[:, :, :], ALU.max).then_inc(max_done, 1)
                        wait(dve, max_done, 1, i, 1)
                        nc.vector.tensor_tensor(d_self[:, :, :], s_self[:, :, :], s_max[:, :, :], ALU.subtract
                                                ).then_inc(d_self_done, 1)
                elif name == "mT":
                    wait_filled(dve, i, name)
                    rows = front_psum(name)[0:H, 0:S]
                    linkf(nc.vector.tensor_scalar(max_rows[:, 0, :], rows, -1.0, None, ALU.mult))
                    nc.vector.scalar_tensor_tensor(max_rows[:, 1, :], rows, -1.0, max_rows[:, 0, :].bitcast(F32),
                                                   ALU.mult, ALU.subtract).then_inc(freed_dve, 1)
                elif name in ("E8", "pvend"):
                    half = 0 if name == "E8" else 1
                    wait(dve, pv_done, H, i, HALF * (half + 1))
                    wait(dve, p_self_done, 1, i, 1)
                    heads = slice(HALF * half, HALF * (half + 1))
                    for t in range(C):
                        sums = pv_bank[t][:, 0:HALF * VW].rearrange("p (h w) -> p h w", w=VW)
                        nc.vector.tensor_reduce(att[:, t, HALF * DH * half:HALF * DH * (half + 1)].rearrange("p (h d) -> p h d", d=DH),
                                                sums[:, :, 0:3 * DH].rearrange("p h (g d) -> p h d g", g=3), AX_X, ALU.add)
                        last = nc.vector.tensor_tensor(den[:, t, heads], sums[:, :, 3 * DH], p_self[:, t, heads], ALU.add)
                    last.then_inc(pv_freed, 1)
                    if half == 1:
                        wait(dve, pv_freed, 2, i, 2)
                        own = v_self[:, :, :].rearrange("p t (h d) -> p (t h) d", d=DH)
                        sums = att[:, :, :].rearrange("p t (h d) -> p (t h) d", d=DH)
                        flat = [P, C * H, DH]
                        linkf(nc.vector.tensor_tensor(own, own, p_self[:, :, :].rearrange("p t h -> p (t h)").unsqueeze(2).to_broadcast(flat),
                                                      ALU.mult))
                        nc.vector.reciprocal(den[:, :, :], den[:, :, :])
                        linkf(nc.vector.tensor_tensor(sums, sums, own, ALU.add))
                        nc.vector.tensor_tensor(sums, sums, den[:, :, :].rearrange("p t h -> p (t h)").unsqueeze(2).to_broadcast(flat),
                                                ALU.mult).then_inc(att_done, 1)
                elif name == "aT":
                    lo_part(i, name, s_hi, s_lo).then_inc(freed_dve, 1)
                elif name == "wo":
                    wait_filled(dve, i, name)
                    for c in range(C):
                        last = nc.vector.scalar_tensor_tensor(x3T[:, c, :], psum[:, c, :], vec[:, c, BO:BO + 1], x2T[:, c, :],
                                                              ALU.add, ALU.add)
                    last.then_inc(freed_dve, 1)
                    wait_freed_dve(dve, i, name)
                    split(x3T, x3_hi, x3_lo).then_inc(x3_split, 1)

            def experts(name, j):
                def linke(ins):
                    link(ins, expert_link, EXPERT_LINKS, j)

                if name[1:].isdigit() and name[0] == "L":
                    s = int(name[1:])
                    wait(dve, hid_hi_done, LSTEPS, j, s + 1)
                    nc.vector.scalar_tensor_tensor(hid_lo[:, s % 2, :], hid_bank[s % 2][:, :], 0.0,
                                                   hid_hi[:, s % 2, :].bitcast(F32), ALU.max, ALU.subtract).then_inc(hid_split, 1)
                elif name == "gate":
                    wait(dve, gate_done, 1, j, 1)
                    nc.vector.tensor_scalar(gate_h[:, :, :], out_bank[0][:, 0:C].unsqueeze(2).to_broadcast([P, C, P]), 0.0, None,
                                            ALU.max).then_inc(gate_relu, 1)
                elif name == "logits":
                    wait(dve, logits_done, 1, j, 1)
                    linke(nc.vector.tensor_reduce(gate_s[:, 0:1], out_bank[1][:, 0:3], AX_X, ALU.max))
                    nc.vector.tensor_scalar(gate_s[:, 1:4], out_bank[1][:, 0:3], gate_s[:, 0:1], None, ALU.subtract
                                            ).then_inc(logits_read, 1)
                elif name == "mix":
                    wait(dve, gate_exp, 1, j, 1)
                    linke(nc.vector.tensor_reduce(gate_s[:, 7:8], gate_s[:, 4:7], AX_X, ALU.add))
                    linke(nc.vector.reciprocal(gate_s[:, 8:9], gate_s[:, 7:8]))
                    linke(nc.vector.tensor_scalar(gate_s[:, 9:12], gate_s[:, 4:7], gate_s[:, 8:9], None, ALU.mult))
                    y = e_out[:, CHOSEN, :, :]
                    linke(nc.vector.scalar_tensor_tensor(y, y, gate_s[:, 9:10], x3T[:, :, :], ALU.mult, ALU.add))
                    linke(nc.vector.scalar_tensor_tensor(y, e_out[:, 0, :, :], gate_s[:, 10:11], y, ALU.mult, ALU.add))
                    nc.vector.scalar_tensor_tensor(y, e_out[:, 1, :, :], gate_s[:, 11:12], y, ALU.mult, ALU.add).then_inc(mixed, 1)

            def turn(names, i, j):
                linked.clear()
                for name in names:
                    if name in EXPERTS:
                        experts(name, j)
                    else:
                        front(name, i)
                assert linked.get(front_link, FRONT_LINKS) == FRONT_LINKS, linked
                assert linked.get(expert_link, EXPERT_LINKS) == EXPERT_LINKS, linked

            dve.wait_ge(lin_in, 64)
            nc.vector.tensor_copy(lin_hi[:, :, :].rearrange("p n f -> p (n f)"), raw[:, :]).then_inc(consts_set, 1)
            dve.wait_ge(consts_set, 1)
            nc.vector.tensor_tensor(lin_lo[:, :, :].rearrange("p n f -> p (n f)"), raw[:, :],
                                    lin_hi[:, :, :].rearrange("p n f -> p (n f)").bitcast(F32), ALU.subtract).then_inc(lin_split, 1)
            dve.wait_ge(consts_in, 16 * 11)
            nc.vector.tensor_copy(lap_mats[:, :], e_out[:, 0, :, :].rearrange("p c t -> p (c t)")).then_inc(consts_set, 1)
            nc.vector.tensor_copy(len_f[:, :], len_sb[:, :]).then_inc(consts_set, 1)
            dve.wait_ge(consts_set, 3)
            nc.vector.tensor_scalar(mask_rows[:, :], iota_sb[:, :], len_f[:, :], MASKED, ALU.is_ge, ALU.mult).then_inc(mask_set, 1)
            dve.wait_ge(bias_done, 1)
            nc.vector.tensor_tensor(ebias[:, 0, :], pv_bank[0][:, 0:2], vec[:, :, BQ], ALU.add)
            nc.vector.tensor_tensor(ebias[:, 1, :], pv_bank[0][:, 3:6:2], vec[:, :, BK], ALU.add)
            nc.vector.tensor_tensor(ebias[:, 2, :], pv_bank[0][:, 2:6:2], vec[:, :, BK], ALU.add).then_inc(consts_set, 1)
            dve.wait_ge(consts_set, 4)
            turn(FRONT, 0, None)
            with dve.Fori(1, B) as i:
                turn(BOTH, i, i - 1)
            turn(EXPERTS, None, B - 1)

        @block.gpsimd
        def _(pool):
            def split_shared(n):
                pool.wait_ge(raw_in, 16 * (n + 1))
                cols = slice((n % 2) * C * F, (n % 2 + 1) * C * F)
                nc.gpsimd.tensor_copy(exp_hi[:, n // 2, cols], raw[:, :]).then_inc(w_hi_done, 1)
                pool.wait_ge(w_hi_done, n + 1)
                nc.gpsimd.tensor_tensor(exp_lo[:, n // 2, cols], raw[:, :], exp_hi[:, n // 2, cols].bitcast(F32),
                                        ALU.subtract).then_inc(w_split, 1)

            def split_chosen(n, j):
                wait(pool, chosen_hi, 2, j, n + 1)
                cols = slice(n * C * F, (n + 1) * C * F)
                nc.gpsimd.tensor_tensor(exp_lo[:, CHOSEN, cols], raw[:, :], exp_hi[:, CHOSEN, cols].bitcast(F32),
                                        ALU.subtract).then_inc(w_split, 1)

            def front(name, i, first):
                if first and name in ("xT", "sT"):
                    split_shared(("xT", "sT").index(name))
                elif name == "xT":
                    split_chosen(0, i - 1)
                elif name == "q" and not first:
                    split_chosen(1, i - 1)
                elif name == "vp":
                    wait(pool, v_hi, 1, i, 1)
                    for t in range(C):
                        v = v_prev[:, t, :].rearrange("p (h d) -> p h d", d=DH)
                        rest = v_rest[:, t, :].rearrange("p (h d) -> p h d", d=DH)
                        part = [v_cols[:, t, :, n * DH:(n + 1) * DH] for n in range(3)]
                        nc.gpsimd.tensor_tensor(part[1], v, part[0], ALU.subtract)
                        nc.gpsimd.tensor_tensor(rest, v, part[0], ALU.subtract).then_inc(v_link, 1)
                        wait(pool, v_link, C, i, t + 1)
                        last = nc.gpsimd.tensor_tensor(part[2], rest, part[1], ALU.subtract)
                    last.then_inc(v_split, 1)
                    if first:
                        split_shared(2)
                elif name == "S8" and first:
                    split_shared(3)
                elif name[0] == "E":
                    h = int(name[1:])
                    wait_freed_act(pool, i, name)
                    nc.gpsimd.tensor_tensor(prob_lo[:, h % 2, :], prob[:, h % 2, :], prob_hi[:, h % 2, :],
                                            ALU.subtract).then_inc(prob_split, 1)

            nc.gpsimd.memset(q_rows[:, :, :].bitcast(F32), 1.0).then_inc(rows_set, 1)
            nc.gpsimd.memset(k_rows[:, :, :].bitcast(F32), 1.0).then_inc(rows_set, 1)
            nc.gpsimd.memset(v_cols[:, :, :, :], 1.0).then_inc(rows_set, 1)
            pool.wait_ge(rows_set, 3)
            for name in FRONT:
                front(name, 0, True)
            with pool.Fori(1, B) as i:
                for name in FRONT:
                    front(name, i, False)
            split_chosen(0, B - 1)
            split_chosen(1, B - 1)


def kernel(**inputs):
    import concourse.bacc as bacc
    from concourse.bass_utils import run_bass_kernel_spmd as run

    a = {k: np.ascontiguousarray(v) for k, v in inputs.items()}
    order = [8 * c + 4 * e + n for e in range(2) for c in range(2) for n in range(4)]
    v_perm = np.array([h * DH + d for h in order for d in range(DH)])
    qk_perm = np.array([P * c + 64 * e + DH * n + d for c in range(2) for e in range(2) for d in range(DH) for n in range(4)])
    wqkvo = np.stack([a["L2_cond_Wq"][:, qk_perm], a["L2_cond_Wk"][:, qk_perm], a["L2_cond_Wv"][:, v_perm],
                      a["L2_cond_Wo"][v_perm, :]])

    def by_partition(v):
        return v.reshape(C, P).T

    vecs = np.stack([by_partition(v) for v in (a["L2_cond_bq"][qk_perm], a["L2_cond_bk"][qk_perm], a["L2_cond_bo"],
                                               a["L2_cond_b_prev"].reshape(D), a["L2_cond_b_self"].reshape(D))], axis=2)
    lap = np.zeros((D, D), np.float32)
    for m in range(D):
        lap[m, m] = -2.0
        for k in (m - 1, m + 1):
            lap[k if 0 <= k < D else 2 * m - k, m] += 1.0
    ones = np.zeros((P, C, H), np.float32)
    for c in range(C):
        for m in range(P):
            ones[m, c, (m // 64) * HALF + 4 * c + m % 4] = 1.0
    consts = np.concatenate([np.eye(P, dtype=np.float32), lap[0:P, 0:P], lap[P:, P:], lap[P:, 0:P], lap[0:P, P:],
                             ones.reshape(P, C * H)], axis=1)
    iota = np.tile(np.arange(S, dtype=np.float32), (B, 1))

    arrays = {
        "x": a["x"], "side": a["fside_BxSxS_0"], "seq_len": a["itok_B_18_1004"].reshape(B, 1),
        "subject": a["itok_B_0_7"].reshape(1, B), "label": a["itok_B_0_2"].reshape(1, B),
        "z": np.stack([a["condB_zX"], a["condB_zY"], a["condB_zR"]], axis=1),
        "w0": a["L0_cond_weight"], "b0": a["L0_cond_bias"].reshape(-1, C, P).transpose(0, 2, 1),
        "wqkvo": wqkvo, "vecs": vecs, "bv": a["L2_cond_bv"][v_perm].reshape(1, D),
        "wi": a["L3_cond_wi"], "wo": a["L3_cond_wo"], "swi": a["L3_cond_swi"], "swo": a["L3_cond_swo"],
        "g1": a["L3_cond_g1"], "g2": a["L3_cond_g2"], "consts": consts, "iota": iota,
    }
    arrays = {f"in_{k}": np.ascontiguousarray(v) for k, v in arrays.items()}
    nc = bacc.Bacc("TRN2", target_bir_lowering=False, num_devices=1, dynamic_dma_scratch_size=1024)
    args = [nc.dram_tensor(k, v.shape, mybir.dt.from_np(v.dtype), kind="ExternalInput").ap() for k, v in arrays.items()]
    out = nc.dram_tensor("out", (B, S, D), F32, kind="ExternalOutput").ap()
    build(nc, *args, out)
    return run(nc, [arrays], core_ids=[0]).results[0]["out"]
```

```python
from contextlib import ExitStack

import numpy as np

import concourse.bass as bass
from concourse import mybir

ALU = mybir.AluOpType
ACT = mybir.ActivationFunctionType
F32 = mybir.dt.float32
F32R = mybir.dt.float32r
BF16 = mybir.dt.bfloat16
F16 = mybir.dt.float16
I32 = mybir.dt.int32
AX_X = mybir.AxisListType.X

P = 128
B = 16
S = 256
D = 256
C = D // P
H = 16
DH = D // H
SCALE = 1.0 / DH ** 0.5
HALF = H // 2
F = 1024
FC = F // P
NE = 3
CHOSEN = 2
STEPS = 4
LSTEPS = NE * STEPS
VW = 3 * DH + 1
ROWS_MAX = 3 * DH + 1
ROWS_EXP = ROWS_MAX + 2
MASKED = -1.0e30

USES = (["xT", "wT", "sT", "x1", "ks", "q", "lap", "vs", "self", "kp", "vp"]
        + [f"S{h}" for h in range(H)] + ["mT"] + [f"E{h}" for h in range(H)])
USE = {name: n for n, name in enumerate(USES)}
NU = len(USES)
assert NU % 2 == 0
ACT_FREES = {"ks"} | {f"E{h}" for h in range(H)}
N_ACT = [sum(x in ACT_FREES for x in USES[:u + 1]) for u in range(NU)]
def own_order(names):
    return [x for name in names if name != "q" for x in ([name, "q"] if name == "lap" else [name])]


DVE_ORDER = [x for x in own_order(USES) if x not in ACT_FREES]
N_DVE = [DVE_ORDER.index(x) + 1 if x in DVE_ORDER else None for x in USES]
DVE_USES = len(DVE_ORDER)
HI_OF = {name: n + 1 for n, name in enumerate(["xT", "wT", "sT", "q", "kp"])}
NHI = len(HI_OF)

FRONT = USES + ["pvend"]
REST = ["aT", "wo"] + [f"L{s}" for s in range(LSTEPS)] + ["Lend", "gate", "logits", "mix", "out0", "out1"]
AFTER = {"sT": ["aT"], "lap": ["wo"], "vp": ["L0", "L1"], "S3": ["L2"], "S7": ["L3"], "S11": ["L4"], "S15": ["L5"],
         "mT": ["L6", "L7"], "E1": ["L8"], "E3": ["L9"], "E5": ["L10"], "E7": ["L11"], "E9": ["Lend"],
         "E10": ["gate"], "E12": ["logits"], "E13": ["mix"], "pvend": ["out0", "out1"]}
BOTH = [x for stage in FRONT for x in [stage] + AFTER.get(stage, [])]
assert [x for x in BOTH if x in REST] == REST
NPROB = 3
DVE_LO = [h for h in range(H) if h % 2]
N_LO_DVE = [sum(g in DVE_LO for g in range(h + 1)) for h in range(H)]
N_LO_POOL = [h + 1 - N_LO_DVE[h] for h in range(H)]

BQ, BK, BO, B_PREV, B_SELF, NVEC = range(6)
FRONT_LINKS = 10
REST_LINKS = 8


def wait(eng, sem, per_turn, turn, n):
    value = turn * per_turn + n
    if isinstance(value, int) and value <= 0:
        return
    eng.wait_ge(sem, value)


def build(nc, x, side, seq_len, subject, label, z, w0, b0, wqkvo, vecs, bv, wi, wo, swi, swo,
          g1, g2, consts, iota, out):
    with ExitStack() as ctx:
        def sb(name, shape, dt=F32):
            return ctx.enter_context(nc.sbuf_tensor(name, shape, dt))

        def bank(name):
            return ctx.enter_context(nc.psum_tensor(name, [P, 512], F32))

        def sem(name):
            return ctx.enter_context(nc.semaphore(name))

        exp_hi = sb("exp_hi", [P, NE, 2 * C * F], F32R)
        exp_lo = sb("exp_lo", [P, NE, 2 * C * F], F32R)
        raw = sb("raw", [P, C * F])
        lin_hi = sb("lin_hi", [P, 4, C * D], F32R)
        lin_lo = sb("lin_lo", [P, 4, C * D], F32R)
        gate1 = sb("gate1", [P, NE * C, D])
        gate2 = sb("gate2", [P, C, 3])
        ident = sb("ident", [P, P])
        head_ones = sb("head_ones", [P, C * H])
        lap_mats = sb("lap_mats", [P, 4 * P], F32R)
        vec = sb("vec", [P, C, NVEC])
        bv_row = sb("bv_row", [P, D])
        ebias = sb("ebias", [P, 3, C])
        iota_sb = sb("iota_sb", [B, S])
        len_sb = sb("len_sb", [B, 1], I32)
        len_f = sb("len_f", [B, 1])
        mask_rows = sb("mask_rows", [B, S], F32R)
        subject_sb = sb("subject_sb", [1, B], I32)
        label_sb = sb("label_sb", [1, B], I32)

        x_nat = sb("x_nat", [P, C, D])
        s_nat = sb("s_nat", [P, C, D])
        w0_nat = sb("w0_nat", [P, C, D])
        b0_sb = sb("b0_sb", [P, C])
        z_sb = sb("z_sb", [P, 3])
        z_neg = sb("z_neg", [P, 1])
        z_one = sb("z_one", [P, 1])
        x1T = sb("x1T", [P, C, S])
        att = sb("att", [P, C, D])
        att_hi = sb("att_hi", [P, C, S], F32R)
        att_lo = sb("att_lo", [P, C, S], F32R)
        x_hi = sb("x_hi", [P, C, S], F32R)
        x_lo = sb("x_lo", [P, C, S], F32R)
        s_hi = sb("s_hi", [P, C, S], F32R)
        s_lo = sb("s_lo", [P, C, S], F32R)
        p_hi = sb("p_hi", [P, C, S], F32R)
        p_lo = sb("p_lo", [P, C, S], F32R)
        ksT = sb("ksT", [P, C, S])
        lapy = sb("lapy", [P, C, S])
        v_prev = lapy
        v_rest = x1T
        x2T = sb("x2T", [P, C, S])
        x3T = sb("x3T", [P, C, S])
        x3_hi = sb("x3_hi", [P, C, S], F32R)
        x3_lo = sb("x3_lo", [P, C, S], F32R)
        q_rows = sb("q_rows", [P, HALF, S], F32R)
        k_rows = sb("k_rows", [P, HALF, S], F32R)
        v_self = sb("v_self", [P, C, D])
        v_cols = sb("v_cols", [P, C, H, VW], BF16)
        s_self = sb("s_self", [P, C, H])
        s_max = sb("s_max", [P, C, H])
        d_self = sb("d_self", [P, C, H])
        p_self = sb("p_self", [P, C, H])
        max_rows = sb("max_rows", [H, 2, S], F32R)
        prob = sb("prob", [P, NPROB, 2 * S])
        prob_hi = sb("prob_hi", [P, NPROB, 2 * S], F16)
        prob_lo = sb("prob_lo", [P, NPROB, 2 * S], F16)
        den = sb("den", [P, C, H])

        hid_hi = sb("hid_hi", [P, 2, 2 * S], F32R)
        hid_lo = sb("hid_lo", [P, 2, 2 * S], F32R)
        e_out = sb("e_out", [P, NE, C, S])
        react = e_out[:, 0, :, :]
        gate_h = sb("gate_h", [P, C, P])
        gate_s = sb("gate_s", [P, 12])
        out_nat = sb("out_nat", [P, C, D])

        mask_dram = nc.dram_tensor("mask_scratch", (B, S), F32R, kind="Internal").ap()

        front_bank = [bank("front0"), bank("front1")]
        pv_bank = [bank("pv0"), bank("pv1")]
        hid_bank = [bank("hid0"), bank("hid1")]
        out_bank = [bank("out0"), bank("out1")]

        consts_in = sem("consts_in")
        lin_in = sem("lin_in")
        consts_set = sem("consts_set")
        bias_done = sem("bias_done")
        mask_set = sem("mask_set")
        rows_set = sem("rows_set")
        lin_split = sem("lin_split")
        x_in = sem("x_in")
        s_in = sem("s_in")
        w0_in = sem("w0_in")
        small_in = sem("small_in")
        raw_in = sem("raw_in")
        filled = sem("filled")
        freed_act = sem("freed_act")
        freed_dve = sem("freed_dve")
        hi_done = sem("hi_done")
        x1_split = sem("x1_split")
        x2_split = sem("x2_split")
        x3_split = sem("x3_split")
        q_placed = sem("q_placed")
        k_placed = sem("k_placed")
        mask_placed = sem("mask_placed")
        max_placed = sem("max_placed")
        v_hi = sem("v_hi")
        v_link = sem("v_link")
        v_split = sem("v_split")
        max_done = sem("max_done")
        d_self_done = sem("d_self_done")
        p_self_done = sem("p_self_done")
        prob_split_dve = sem("prob_split_dve")
        prob_split_pool = sem("prob_split_pool")
        pv_done = sem("pv_done")
        pv_freed = sem("pv_freed")
        att_done = sem("att_done")
        front_link = sem("front_link")
        att_turned = sem("att_turned")
        att_hi_done = sem("att_hi_done")
        att_split = sem("att_split")
        wo_done = sem("wo_done")
        w_hi_done = sem("w_hi_done")
        w_split = sem("w_split")
        chosen_hi = sem("chosen_hi")
        hid_filled = sem("hid_filled")
        hid_hi_done = sem("hid_hi_done")
        hid_split = sem("hid_split")
        step_done = sem("step_done")
        e_out_done = sem("e_out_done")
        gate_done = sem("gate_done")
        gate_relu = sem("gate_relu")
        logits_done = sem("logits_done")
        logits_read = sem("logits_read")
        gate_exp = sem("gate_exp")
        mixed = sem("mixed")
        out_copied = sem("out_copied")
        stored = sem("stored")
        rest_link = sem("rest_link")

        def front_psum(name):
            return front_bank[USE[name] % 2]

        def chunked(t):
            return t[:, :].rearrange("p (c t) -> p c t", c=C)

        def wait_filled(eng, i, name):
            wait(eng, filled, NU, i, USE[name] + 1)

        def wait_freed_dve(eng, i, name):
            wait(eng, freed_dve, DVE_USES, i, N_DVE[USE[name]])

        def wait_freed_act(eng, i, name):
            wait(eng, freed_act, N_ACT[-1], i, N_ACT[USE[name]])

        def wait_prob_split(eng, i, h):
            if h in DVE_LO:
                wait(eng, prob_split_dve, N_LO_DVE[-1], i, N_LO_DVE[h])
            elif h >= 0:
                wait(eng, prob_split_pool, N_LO_POOL[-1], i, N_LO_POOL[h])

        def expert_w(part, e):
            w_in = part[:, e, 0:C * F].rearrange("p (k f) -> p k f", k=C)
            w_out = part[:, e, C * F:2 * C * F].rearrange("p (f d) -> p f d", d=D)
            return w_in, w_out

        block = ctx.enter_context(nc.Block())

        @block.sync
        def _(sp):
            def load_x(b):
                sp.dma_start(x_nat[:, :, :], x[bass.ds(b, 1)].rearrange("o (n p) d -> p (o n) d", p=P)).then_inc(x_in, 16)

            def load_s(b):
                sp.dma_start(s_nat[:, :, :], side[bass.ds(b, 1)].rearrange("o (n p) d -> p (o n) d", p=P)).then_inc(s_in, 16)

            def chooser(row, b, count):
                return sp.value_load(row[0:1, bass.ds(b, 1)], min_val=0, max_val=count - 1)

            def load_w0(who):
                sp.dma_start(w0_nat[:, :, :], w0[bass.ds(who, 1)].rearrange("o (n p) h -> p (o n) h", p=P)).then_inc(w0_in, 16)

            def load_small(b, who):
                sp.dma_start(b0_sb[:, :], b0[bass.ds(who, 1)].rearrange("o p c -> (o p) c")).then_inc(small_in, 16)
                sp.dma_start(z_sb[:, :], z[bass.ds(b, 1)].to_broadcast([P, 3])).then_inc(small_in, 16)

            def load_wi(kind):
                sp.dma_start(raw[:, :].rearrange("p (k f) -> p k f", k=C),
                             wi[bass.ds(kind, 1)].rearrange("o (k p) f -> p (o k) f", p=P)).then_inc(raw_in, 16)

            def load_wo(kind):
                sp.dma_start(raw[:, :].rearrange("p (f d) -> p f d", d=D),
                             wo[bass.ds(kind, 1)].rearrange("o (f p) d -> p (o f) d", p=P)).then_inc(raw_in, 16)

            def load_shared(n):
                if n % 2 == 0:
                    sp.dma_start(raw[:, :].rearrange("p (k f) -> p k f", k=C),
                                 swi[n // 2].rearrange("(k p) f -> p k f", p=P)).then_inc(raw_in, 16)
                else:
                    sp.dma_start(raw[:, :].rearrange("p (f d) -> p f d", d=D),
                                 swo[n // 2].rearrange("(f p) d -> p f d", p=P)).then_inc(raw_in, 16)

            def place(rows, part, first_row, done):
                for e in range(2):
                    sp.dma_start(rows[64 * e + first_row:64 * e + first_row + DH, :, :].bitcast(F32),
                                 part[64 * e:64 * e + 64, :, :].bitcast(F32)).then_inc(done, 16)

            def stage(name, i, first):
                nxt = (i + 1) % B
                if name in REST:
                    return
                if name == "xT":
                    wait_filled(sp, i, "xT")
                    load_x(nxt)
                    sp.dma_start(k_rows[3 * DH:64 + 3 * DH + 1:64, :, :].bitcast(F32),
                                 mask_dram[bass.ds(i, 1), :].bitcast(F32).unsqueeze(1).to_broadcast([2, HALF, S])
                                 ).then_inc(mask_placed, 16)
                elif name == "wT":
                    who = chooser(subject_sb, nxt, w0.shape[0])
                    wait_filled(sp, i, "wT")
                    load_w0(who)
                elif name == "sT":
                    wait_filled(sp, i, "sT")
                    load_s(nxt)
                    if first:
                        sp.wait_ge(w_split, 1)
                        load_shared(1)
                elif name == "q":
                    wait_freed_dve(sp, i, "q")
                    place(q_rows, p_hi, 0, q_placed)
                    place(q_rows, p_lo, DH, q_placed)
                    place(q_rows, p_hi, 2 * DH, q_placed)
                    if first:
                        sp.wait_ge(w_split, 2)
                        load_shared(2)
                elif name == "kp":
                    who = chooser(subject_sb, nxt, w0.shape[0])
                    wait(sp, x2_split, 1, i, 1)
                    load_small(nxt, who)
                    wait_freed_dve(sp, i, "kp")
                    place(k_rows, p_hi, 0, k_placed)
                    place(k_rows, p_hi, DH, k_placed)
                    place(k_rows, p_lo, 2 * DH, k_placed)
                elif name == "vp" and first:
                    sp.wait_ge(w_split, 3)
                    load_shared(3)
                elif name == "S1" and not first:
                    kind = chooser(label_sb, i - 1, wo.shape[0])
                    wait(sp, w_split, 2, i - 1, 5)
                    load_wo(kind)
                elif name == "mT":
                    wait_freed_dve(sp, i, "mT")
                    for j in range(2):
                        row = ROWS_MAX + j
                        sp.dma_start(q_rows[row:64 + row + 1:64, :, :].bitcast(F32),
                                     max_rows[:, j, :].bitcast(F32)).then_inc(max_placed, 16)
                elif name == "E2":
                    kind = chooser(label_sb, i, wi.shape[0])
                    wait(sp, w_split, 2, i, 4)
                    load_wi(kind)

            def store(j):
                wait(sp, out_copied, C, j, C)
                sp.dma_start(out[bass.ds(j, 1)].rearrange("o (n p) d -> p (o n) d", p=P), out_nat[:, :, :]).then_inc(stored, 16)

            sp.dma_start(subject_sb[:, :], subject).then_inc(consts_in, 16)
            sp.dma_start(label_sb[:, :], label).then_inc(consts_in, 16)
            sp.dma_start(ident[:, :], consts[:, 0:P]).then_inc(consts_in, 16)
            load_x(0)
            sp.wait_ge(consts_in, 48)
            load_w0(chooser(subject_sb, 0, w0.shape[0]))
            load_s(0)
            load_small(0, chooser(subject_sb, 0, w0.shape[0]))
            for n in range(4):
                sp.dma_start(raw[:, n * C * D:(n + 1) * C * D].rearrange("p (k f) -> p k f", k=C),
                             wqkvo[n].rearrange("(k p) f -> p k f", p=P)).then_inc(lin_in, 16)
            sp.dma_start(vec[:, :, :], vecs).then_inc(consts_in, 16)
            sp.dma_start(e_out[:, 0, :, :].rearrange("p c t -> p (c t)"), consts[:, P:5 * P]).then_inc(consts_in, 16)
            sp.dma_start(head_ones[:, :], consts[:, 5 * P:5 * P + C * H]).then_inc(consts_in, 16)
            sp.dma_start(iota_sb[:, :], iota).then_inc(consts_in, 16)
            sp.dma_start(len_sb[:, :], seq_len).then_inc(consts_in, 16)
            sp.dma_start(bv_row[:, :], bv.to_broadcast([P, D])).then_inc(consts_in, 16)
            sp.dma_start(gate1[:, :, :], g1.rearrange("(k p) f -> p k f", p=P)).then_inc(consts_in, 16)
            sp.dma_start(gate2[:, :, :], g2.rearrange("(k p) f -> p k f", p=P)).then_inc(consts_in, 16)
            sp.wait_ge(mask_set, 1)
            sp.dma_start(mask_dram.bitcast(F32), mask_rows[:, :].bitcast(F32)).then_inc(stored, 16)
            sp.wait_ge(stored, 16)
            sp.wait_ge(lin_split, 1)
            sp.wait_ge(bias_done, 1)
            load_shared(0)
            sp.wait_ge(rows_set, 2)
            for name in FRONT:
                stage(name, 0, True)
            with sp.Fori(1, B) as i:
                for name in BOTH:
                    if name == "out1":
                        store(i - 1)
                    else:
                        stage(name, i, False)
            kind = chooser(label_sb, B - 1, wo.shape[0])
            wait(sp, w_split, 2, B - 1, 5)
            load_wo(kind)
            store(B - 1)
            sp.wait_ge(x_in, 16 * (B + 1))
            sp.wait_ge(s_in, 16 * (B + 1))
            sp.wait_ge(w0_in, 16 * (B + 1))
            sp.wait_ge(small_in, 32 * (B + 1))
            sp.wait_ge(stored, 16 * (B + 1))

        @block.tensor
        def _(pe):
            def product(acc, w_hi, w_lo, a_hi, a_lo, first, last):
                nc.tensor.matmul(acc, w_hi, a_hi, start=first, stop=False)
                nc.tensor.matmul(acc, w_hi, a_lo, start=False, stop=False)
                return nc.tensor.matmul(acc, w_lo, a_hi, start=False, stop=last)

            def linear(n):
                return (lin_hi[:, n, :].rearrange("p (k f) -> p k f", k=C),
                        lin_lo[:, n, :].rearrange("p (k f) -> p k f", k=C))

            def feature_major(psum, w, a_hi, a_lo):
                for c in range(C):
                    for k in range(C):
                        last = product(psum[:, c * S:(c + 1) * S], w[0][:, k, c * P:(c + 1) * P],
                                       w[1][:, k, c * P:(c + 1) * P], a_hi[:, k, :], a_lo[:, k, :], k == 0, k == C - 1)
                return last

            def token_major(psum, w, a_hi, a_lo):
                for t in range(C):
                    for k in range(C):
                        last = product(psum[:, t * D:(t + 1) * D], a_hi[:, k, t * P:(t + 1) * P],
                                       a_lo[:, k, t * P:(t + 1) * P], w[0][:, k, :], w[1][:, k, :], k == 0, k == C - 1)
                return last

            def transposed(psum, src):
                for c in range(C):
                    for t in range(C):
                        last = nc.tensor.transpose(psum[:, c * S + t * P:c * S + (t + 1) * P],
                                                   src[:, t, c * P:(c + 1) * P], ident[:, :])
                return last

            def open_bank(i, name):
                u, turn = USE[name] - 2, i
                if u < 0:
                    u, turn = u + NU, i - 1
                (wait_freed_act if USES[u] in ACT_FREES else wait_freed_dve)(pe, turn, USES[u])
                return front_bank[USE[name] % 2]

            def attend(i, h):
                wait_prob_split(pe, i, h)
                if h == 0:
                    wait(pe, v_split, 1, i, 1)
                if h == HALF:
                    wait(pe, pv_freed, 2, i, 1)
                for t in range(C):
                    acc = pv_bank[t][:, (h % HALF) * VW:(h % HALF + 1) * VW]
                    for k in range(C):
                        at = k * S + t * P
                        nc.tensor.matmul(acc, prob_hi[:, h % NPROB, at:at + P], v_cols[:, k, h, :], start=(k == 0), stop=False)
                        last = nc.tensor.matmul(acc, prob_lo[:, h % NPROB, at:at + P], v_cols[:, k, h, :],
                                                start=False, stop=(k == C - 1))
                last.then_inc(pv_done, 1)

            def front(name, i):
                if name == "pvend":
                    attend(i, H - 2)
                    attend(i, H - 1)
                    return
                psum = open_bank(i, name)
                if name == "xT":
                    wait(pe, x_in, 16, i, 16)
                    last = transposed(psum, x_nat)
                elif name == "wT":
                    wait(pe, w0_in, 16, i, 16)
                    last = transposed(psum, w0_nat)
                elif name == "sT":
                    wait(pe, s_in, 16, i, 16)
                    last = transposed(psum, s_nat)
                elif name == "x1":
                    wait_freed_dve(pe, i, "wT")
                    last = feature_major(psum, (p_hi, p_lo), x_hi, x_lo)
                elif name == "ks":
                    wait_freed_dve(pe, i, "sT")
                    last = feature_major(psum, linear(1), s_hi, s_lo)
                elif name == "q":
                    last = feature_major(psum, linear(0), s_hi, s_lo)
                elif name == "lap":
                    wait(pe, x1_split, 1, i, 1)
                    for c in range(C):
                        acc = psum[:, c * S:(c + 1) * S]
                        own = lap_mats[:, c * P:(c + 1) * P]
                        across = lap_mats[:, (2 + c) * P:(3 + c) * P]
                        nc.tensor.matmul(acc, own, x_hi[:, c, :], start=True, stop=False)
                        nc.tensor.matmul(acc, own, x_lo[:, c, :], start=False, stop=False)
                        nc.tensor.matmul(acc, across, x_hi[:, 1 - c, :], start=False, stop=False)
                        last = nc.tensor.matmul(acc, across, x_lo[:, 1 - c, :], start=False, stop=True)
                elif name == "vs":
                    last = token_major(psum, linear(2), s_hi, s_lo)
                elif name == "self":
                    wait_freed_dve(pe, i, "q")
                    for t in range(C):
                        for c in range(C):
                            last = nc.tensor.matmul(psum[:, t * H:(t + 1) * H], ksT[:, c, t * P:(t + 1) * P],
                                                    head_ones[:, c * H:(c + 1) * H], start=(c == 0), stop=(c == C - 1))
                elif name == "kp":
                    wait(pe, x2_split, 1, i, 1)
                    last = feature_major(psum, linear(1), x_hi, x_lo)
                elif name == "vp":
                    last = token_major(psum, linear(2), x_hi, x_lo)
                elif name[0] == "S":
                    h = int(name[1:])
                    if h == 0:
                        wait(pe, q_placed, 16 * 6, i, 16 * 6)
                        wait(pe, k_placed, 16 * 6, i, 16 * 6)
                        wait(pe, mask_placed, 16, i, 16)
                    at, slot = 64 * (h // HALF), h % HALF
                    for t in range(C):
                        last = nc.tensor.matmul(psum[:, t * S:(t + 1) * S], q_rows[at:at + ROWS_MAX, slot, t * P:(t + 1) * P],
                                                k_rows[at:at + ROWS_MAX, slot, :], start=True, stop=True)
                elif name == "mT":
                    wait(pe, max_done, 1, i, 1)
                    for t in range(C):
                        last = nc.tensor.transpose(psum[0:H, t * P:(t + 1) * P], s_max[:, t, :], ident[:, :])
                elif name[0] == "E":
                    h = int(name[1:])
                    if h == 0:
                        wait(pe, max_placed, 16 * 2, i, 16 * 2)
                    at, slot = 64 * (h // HALF), h % HALF
                    for k in range(C):
                        last = nc.tensor.matmul(psum[:, k * S:(k + 1) * S], k_rows[at:at + ROWS_EXP, slot, k * P:(k + 1) * P],
                                                q_rows[at:at + ROWS_EXP, slot, :], start=True, stop=True)
                last.then_inc(filled, 1)
                if name[0] == "E" and int(name[1:]) >= 2:
                    attend(i, int(name[1:]) - 2)

            def hidden(s, j):
                e = s // STEPS
                (hi, _), (lo, _) = expert_w(exp_hi, e), expert_w(exp_lo, e)
                if s == 0:
                    wait(pe, x3_split, 1, j, 1)
                    pe.wait_ge(w_split, 4)
                if s == CHOSEN * STEPS:
                    wait(pe, w_split, 2, j, 5)
                if s >= 2:
                    wait(pe, hid_split, LSTEPS, j, s - 1)
                psum = hid_bank[s % 2]
                for f in range(2):
                    at = (2 * (s % STEPS) + f) * P
                    for k in range(C):
                        last = product(psum[:, f * S:(f + 1) * S], hi[:, k, at:at + P], lo[:, k, at:at + P],
                                       x3_hi[:, k, :], x3_lo[:, k, :], k == 0, k == C - 1)
                last.then_inc(hid_filled, 1)

            def project(s, j):
                e = s // STEPS
                (_, hi), (_, lo) = expert_w(exp_hi, e), expert_w(exp_lo, e)
                wait(pe, hid_split, LSTEPS, j, s + 1)
                if s and s % STEPS == 0:
                    wait(pe, e_out_done, NE, j, e)
                if s == CHOSEN * STEPS:
                    wait(pe, w_split, 2, j, 6)
                for f in range(2):
                    n = 2 * (s % STEPS) + f
                    for c in range(C):
                        last = product(out_bank[c][:, 0:S], hi[:, n, c * P:(c + 1) * P], lo[:, n, c * P:(c + 1) * P],
                                       hid_hi[:, s % 2, f * S:(f + 1) * S], hid_lo[:, s % 2, f * S:(f + 1) * S],
                                       n == 0, n == FC - 1)
                last.then_inc(step_done, 1)

            def rest(name, j):
                if name == "aT":
                    wait(pe, att_done, 1, j, 1)
                    transposed(pv_bank[0], att).then_inc(att_turned, 1)
                elif name == "wo":
                    wait(pe, att_split, 1, j, 1)
                    feature_major(pv_bank[1], linear(3), att_hi, att_lo).then_inc(wo_done, 1)
                elif name[1:].isdigit() and name[0] == "L":
                    s = int(name[1:])
                    hidden(s, j)
                    if s:
                        project(s - 1, j)
                elif name == "Lend":
                    project(LSTEPS - 1, j)
                elif name == "gate":
                    wait(pe, e_out_done, NE, j, NE)
                    for c in range(C):
                        for n in range(NE * C):
                            e = (CHOSEN, 0, 1)[n // C]
                            last = nc.tensor.matmul(out_bank[0][:, c:c + 1], gate1[:, n, c * P:(c + 1) * P],
                                                    e_out[:, e, n % C, 0:1], start=(n == 0), stop=(n == NE * C - 1))
                    last.then_inc(gate_done, 1)
                elif name == "logits":
                    wait(pe, gate_relu, 1, j, 1)
                    for c in range(C):
                        last = nc.tensor.matmul(out_bank[1][:, 0:3], gate_h[:, c, :], gate2[:, c, :],
                                                start=(c == 0), stop=(c == C - 1))
                    last.then_inc(logits_done, 1)
                elif name in ("out0", "out1"):
                    t = int(name[3])
                    if t == 0:
                        wait(pe, mixed, 1, j, 1)
                    wait(pe, hid_split, LSTEPS, j, LSTEPS - 1 + t)
                    for c in range(C):
                        last = nc.tensor.transpose(hid_bank[t][:, c * P:(c + 1) * P],
                                                   e_out[:, CHOSEN, c, t * P:(t + 1) * P], ident[:, :])
                    last.then_inc(hid_filled, 1)

            pe.wait_ge(lin_in, 64)
            pe.wait_ge(consts_in, 16 * 11)
            for c in range(C):
                for k in range(C):
                    at = k * D + c * P
                    nc.tensor.matmul(pv_bank[0][:, c:c + 1], raw[:, at:at + P], vec[:, k, B_SELF:B_SELF + 1],
                                     start=(k == 0), stop=(k == C - 1))
            for c in range(C):
                for k in range(C):
                    at = C * D + k * D + c * P
                    last = nc.tensor.matmul(pv_bank[0][:, 2 + 2 * c:4 + 2 * c], raw[:, at:at + P],
                                            vec[:, k, B_PREV:B_PREV + 2], start=(k == 0), stop=(k == C - 1))
            last.then_inc(bias_done, 1)
            pe.wait_ge(consts_set, 4)
            pe.wait_ge(lin_split, 1)
            for name in FRONT:
                front(name, 0)
            with pe.Fori(1, B) as i:
                for name in BOTH:
                    if name in REST:
                        rest(name, i - 1)
                    else:
                        front(name, i)
            for name in REST:
                rest(name, B - 1)

        @block.scalar
        def _(act):
            def round_hi(i, name, dst, bias=None):
                wait_filled(act, i, name)
                psum = chunked(front_psum(name))
                if bias is None:
                    last = nc.scalar.activation(dst[:, :, :], psum, ACT.Copy)
                else:
                    for c in range(C):
                        last = nc.scalar.activation(dst[:, c, :], psum[:, c, :], ACT.Identity, bias=bias[:, c:c + 1])
                last.then_inc(hi_done, 1)

            def front(name, i):
                if name == "xT":
                    wait_filled(act, i, name)
                    nc.scalar.activation(x1T[:, :, :], chunked(front_psum(name)), ACT.Copy)
                    round_hi(i, name, x_hi)
                elif name == "wT":
                    wait(act, k_placed, 16 * 6, i - 1, 16 * 6)
                    round_hi(i, name, p_hi)
                elif name == "sT":
                    round_hi(i, name, s_hi)
                elif name == "ks":
                    wait_filled(act, i, name)
                    psum = chunked(front_psum(name))
                    for c in range(C):
                        last = nc.scalar.activation(ksT[:, c, :], psum[:, c, :], ACT.Identity, bias=ebias[:, 1, c:c + 1])
                    last.then_inc(freed_act, 1)
                elif name == "q":
                    round_hi(i, name, p_hi, ebias[:, 0, :])
                elif name == "kp":
                    wait(act, q_placed, 16 * 6, i, 16 * 6)
                    round_hi(i, name, p_hi, ebias[:, 2, :])
                elif name == "vp":
                    wait_freed_dve(act, i, "vp")
                    wait(act, pv_done, H, i - 1, H)
                    for t in range(C):
                        last = nc.scalar.activation(v_cols[:, t, :, 0:DH], v_prev[:, t, :].rearrange("p (h d) -> p h d", d=DH), ACT.Copy)
                    last.then_inc(v_hi, 1)
                elif name == "mT":
                    wait(act, d_self_done, 1, i, 1)
                    nc.scalar.activation(p_self[:, :, :], d_self[:, :, :], ACT.Exp, scale=SCALE).then_inc(p_self_done, 1)
                elif name[0] == "E":
                    h = int(name[1:])
                    wait_filled(act, i, name)
                    if h >= NPROB:
                        wait_prob_split(act, i, h - NPROB)
                    psum = front_psum(name)
                    nc.scalar.activation(prob[:, h % NPROB, :], psum[:, :], ACT.Exp, scale=SCALE)
                    if h >= NPROB:
                        wait(act, pv_done, H, i, h - NPROB + 1)
                    nc.scalar.activation(prob_hi[:, h % NPROB, :], psum[:, :], ACT.Exp, scale=SCALE).then_inc(freed_act, 1)

            def chosen_hi_part(n, j):
                wait(act, raw_in, 32, j, 16 * (4 + n + 1))
                nc.scalar.activation(exp_hi[:, CHOSEN, n * C * F:(n + 1) * C * F], raw[:, :], ACT.Copy).then_inc(chosen_hi, 1)

            def keep_output(e, j):
                wait(act, step_done, LSTEPS, j, (e + 1) * STEPS)
                for c in range(C):
                    last = nc.scalar.activation(e_out[:, e, c, :], out_bank[c][:, 0:S], ACT.Copy)
                last.then_inc(e_out_done, 1)

            def rest(name, j):
                if name == "aT":
                    wait(act, att_turned, 1, j, 1)
                    nc.scalar.activation(att_hi[:, :, :], chunked(pv_bank[0]), ACT.Copy).then_inc(att_hi_done, 1)
                elif name[1:].isdigit() and name[0] == "L":
                    s = int(name[1:])
                    wait(act, hid_filled, LSTEPS + C, j, s + 1)
                    if s >= 2:
                        wait(act, step_done, LSTEPS, j, s - 1)
                    nc.scalar.activation(hid_hi[:, s % 2, :], hid_bank[s % 2][:, :], ACT.Relu).then_inc(hid_hi_done, 1)
                    if s and s % STEPS == 0:
                        keep_output(s // STEPS - 1, j)
                elif name == "Lend":
                    keep_output(NE - 1, j)
                elif name == "logits":
                    wait(act, logits_read, 1, j, 1)
                    nc.scalar.activation(gate_s[:, 4:7], gate_s[:, 1:4], ACT.Exp).then_inc(gate_exp, 1)
                elif name in ("out0", "out1"):
                    t = int(name[3])
                    wait(act, hid_filled, LSTEPS + C, j, LSTEPS + t + 1)
                    if t == 0:
                        wait(act, stored, 16, j, 16)
                    nc.scalar.activation(out_nat[:, t, :], hid_bank[t][:, 0:D], ACT.Copy).then_inc(out_copied, 1)

            act.wait_ge(consts_set, 4)
            act.wait_ge(rows_set, 3)
            for name in FRONT:
                front(name, 0)
            with act.Fori(1, B) as i:
                for name in BOTH:
                    if name in REST:
                        rest(name, i - 1)
                    else:
                        front(name, i)
                    if name == "vp":
                        chosen_hi_part(0, i - 1)
                    elif name == "S12":
                        chosen_hi_part(1, i - 1)
            chosen_hi_part(0, B - 1)
            for name in REST:
                rest(name, B - 1)
                if name == "L4":
                    chosen_hi_part(1, B - 1)

        @block.vector
        def _(dve):
            linked = {}

            def link(ins, sem_, per_turn, turn):
                linked[sem_] = linked.get(sem_, 0) + 1
                ins.then_inc(sem_, 1)
                wait(dve, sem_, per_turn, turn, linked[sem_])

            def lo_part(i, name, hi, lo, bias=None):
                wait(dve, hi_done, NHI, i, HI_OF[name])
                psum = chunked(front_psum(name))
                if bias is None:
                    return nc.vector.tensor_tensor(lo[:, :, :], psum, hi[:, :, :].bitcast(F32), ALU.subtract)
                for c in range(C):
                    last = nc.vector.scalar_tensor_tensor(lo[:, c, :], psum[:, c, :], bias[:, c:c + 1],
                                                          hi[:, c, :].bitcast(F32), ALU.add, ALU.subtract)
                return last

            def front(name, i):
                def linkf(ins):
                    link(ins, front_link, FRONT_LINKS, i)

                def split(src, hi, lo):
                    linkf(nc.vector.tensor_copy(hi[:, :, :], src[:, :, :]))
                    return nc.vector.tensor_tensor(lo[:, :, :], src[:, :, :], hi[:, :, :].bitcast(F32), ALU.subtract)

                psum = chunked(front_psum(name)) if name in USE else None
                if name == "xT":
                    lo_part(i, name, x_hi, x_lo).then_inc(freed_dve, 1)
                elif name == "wT":
                    lo_part(i, name, p_hi, p_lo).then_inc(freed_dve, 1)
                elif name == "sT":
                    lo_part(i, name, s_hi, s_lo).then_inc(freed_dve, 1)
                elif name == "x1":
                    wait_filled(dve, i, name)
                    wait(dve, small_in, 32, i, 32)
                    nc.vector.tensor_scalar(z_neg[:, :], z_sb[:, 2:3], -1.0, None, ALU.mult)
                    nc.vector.tensor_scalar(z_one[:, :], z_sb[:, 2:3], 1.0, None, ALU.add)
                    nc.vector.scalar_tensor_tensor(x1T[:, 0, :], psum[:, 0, :], b0_sb[:, 0:1], x1T[:, 0, :], ALU.add, ALU.add)
                    nc.vector.scalar_tensor_tensor(x1T[:, 1, :], psum[:, 1, :], b0_sb[:, 1:2], x1T[:, 1, :],
                                                   ALU.add, ALU.add).then_inc(freed_dve, 1)
                    wait_freed_dve(dve, i, name)
                    split(x1T, x_hi, x_lo).then_inc(x1_split, 1)
                    nc.vector.tensor_tensor(lapy[:, :, 1:S - 1], x1T[:, :, 0:S - 2], x1T[:, :, 2:S], ALU.add)
                    linkf(nc.vector.tensor_scalar(lapy[:, :, 0:S:S - 1], x1T[:, :, 1:S - 1:S - 3], 2.0, None, ALU.mult))
                    linkf(nc.vector.scalar_tensor_tensor(lapy[:, :, :], x1T[:, :, :], -2.0, lapy[:, :, :], ALU.mult, ALU.add))
                    linkf(nc.vector.tensor_scalar(react[:, :, :], x1T[:, :, :], z_neg[:, :], z_one[:, :], ALU.mult, ALU.add))
                    linkf(nc.vector.tensor_tensor(react[:, :, :], react[:, :, :], x1T[:, :, :], ALU.mult))
                    linkf(nc.vector.scalar_tensor_tensor(react[:, :, :], lapy[:, :, :], z_sb[:, 1:2], react[:, :, :],
                                                         ALU.mult, ALU.add))
                elif name == "lap":
                    wait_filled(dve, i, name)
                    nc.vector.scalar_tensor_tensor(x2T[:, :, :], psum, z_sb[:, 0:1], react[:, :, :],
                                                   ALU.mult, ALU.add).then_inc(freed_dve, 1)
                    wait_freed_dve(dve, i, name)
                    split(x2T, x_hi, x_lo).then_inc(x2_split, 1)
                elif name == "q":
                    lo_part(i, name, p_hi, p_lo, ebias[:, 0, :])
                    wait_freed_act(dve, i, "ks")
                    for c in range(C):
                        last = nc.vector.scalar_tensor_tensor(ksT[:, c, :], psum[:, c, :], ebias[:, 0, c:c + 1],
                                                              ksT[:, c, :], ALU.add, ALU.mult)
                    last.then_inc(freed_dve, 1)
                elif name == "vs":
                    wait_filled(dve, i, name)
                    for t in range(C):
                        last = nc.vector.tensor_tensor(v_self[:, t, :], psum[:, t, :], bv_row[:, :], ALU.add)
                    last.then_inc(freed_dve, 1)
                elif name == "self":
                    wait_filled(dve, i, name)
                    nc.vector.tensor_copy(s_self[:, :, :], front_psum(name)[:, 0:C * H].rearrange("p (t h) -> p t h", h=H)
                                          ).then_inc(freed_dve, 1)
                elif name == "kp":
                    lo_part(i, name, p_hi, p_lo, ebias[:, 2, :]).then_inc(freed_dve, 1)
                elif name == "vp":
                    wait_filled(dve, i, name)
                    for t in range(C):
                        last = nc.vector.tensor_tensor(v_prev[:, t, :], psum[:, t, :], bv_row[:, :], ALU.add)
                    last.then_inc(freed_dve, 1)
                elif name[0] == "S":
                    h = int(name[1:])
                    wait_filled(dve, i, name)
                    nc.vector.tensor_reduce(s_max[:, :, h:h + 1], psum, AX_X, ALU.max).then_inc(freed_dve, 1)
                    if h == H - 1:
                        wait_freed_dve(dve, i, name)
                        nc.vector.tensor_tensor(s_max[:, :, :], s_max[:, :, :], s_self[:, :, :], ALU.max).then_inc(max_done, 1)
                        wait(dve, max_done, 1, i, 1)
                        nc.vector.tensor_tensor(d_self[:, :, :], s_self[:, :, :], s_max[:, :, :], ALU.subtract
                                                ).then_inc(d_self_done, 1)
                elif name == "mT":
                    wait_filled(dve, i, name)
                    rows = front_psum(name)[0:H, 0:S]
                    linkf(nc.vector.tensor_scalar(max_rows[:, 0, :], rows, -1.0, None, ALU.mult))
                    nc.vector.scalar_tensor_tensor(max_rows[:, 1, :], rows, -1.0, max_rows[:, 0, :].bitcast(F32),
                                                   ALU.mult, ALU.subtract).then_inc(freed_dve, 1)
                if name[0] == "E" and int(name[1:]) in DVE_LO:
                    h = int(name[1:])
                    wait_freed_act(dve, i, name)
                    nc.vector.tensor_tensor(prob_lo[:, h % NPROB, :], prob[:, h % NPROB, :], prob_hi[:, h % NPROB, :],
                                            ALU.subtract).then_inc(prob_split_dve, 1)
                if name in ("E9", "pvend"):
                    half = 0 if name == "E9" else 1
                    wait(dve, pv_done, H, i, HALF * (half + 1))
                    wait(dve, p_self_done, 1, i, 1)
                    heads = slice(HALF * half, HALF * (half + 1))
                    for t in range(C):
                        sums = pv_bank[t][:, 0:HALF * VW].rearrange("p (h w) -> p h w", w=VW)
                        nc.vector.tensor_reduce(att[:, t, HALF * DH * half:HALF * DH * (half + 1)].rearrange("p (h d) -> p h d", d=DH),
                                                sums[:, :, 0:3 * DH].rearrange("p h (g d) -> p h d g", g=3), AX_X, ALU.add)
                        last = nc.vector.tensor_tensor(den[:, t, heads], sums[:, :, 3 * DH], p_self[:, t, heads], ALU.add)
                    last.then_inc(pv_freed, 1)
                    if half == 1:
                        for c in range(C):
                            nc.vector.tensor_scalar(x3T[:, c, :], x2T[:, c, :], vec[:, c, BO:BO + 1], None, ALU.add)
                    if half == 1:
                        wait(dve, pv_freed, 2, i, 2)
                        own = v_self[:, :, :].rearrange("p t (h d) -> p (t h) d", d=DH)
                        sums = att[:, :, :].rearrange("p t (h d) -> p (t h) d", d=DH)
                        flat = [P, C * H, DH]
                        linkf(nc.vector.tensor_tensor(own, own, p_self[:, :, :].rearrange("p t h -> p (t h)").unsqueeze(2).to_broadcast(flat),
                                                      ALU.mult))
                        nc.vector.reciprocal(den[:, :, :], den[:, :, :])
                        linkf(nc.vector.tensor_tensor(sums, sums, own, ALU.add))
                        nc.vector.tensor_tensor(sums, sums, den[:, :, :].rearrange("p t h -> p (t h)").unsqueeze(2).to_broadcast(flat),
                                                ALU.mult).then_inc(att_done, 1)

            def rest(name, j):
                def linke(ins):
                    link(ins, rest_link, REST_LINKS, j)

                if name == "aT":
                    wait(dve, att_hi_done, 1, j, 1)
                    nc.vector.tensor_tensor(att_lo[:, :, :], chunked(pv_bank[0]), att_hi[:, :, :].bitcast(F32),
                                            ALU.subtract).then_inc(att_split, 1)
                elif name == "wo":
                    wait(dve, wo_done, 1, j, 1)
                    linke(nc.vector.tensor_tensor(x3T[:, :, :], chunked(pv_bank[1]), x3T[:, :, :], ALU.add))
                    linke(nc.vector.tensor_copy(x3_hi[:, :, :], x3T[:, :, :]))
                    nc.vector.tensor_tensor(x3_lo[:, :, :], x3T[:, :, :], x3_hi[:, :, :].bitcast(F32), ALU.subtract).then_inc(x3_split, 1)
                elif name[1:].isdigit() and name[0] == "L":
                    s = int(name[1:])
                    wait(dve, hid_hi_done, LSTEPS, j, s + 1)
                    nc.vector.scalar_tensor_tensor(hid_lo[:, s % 2, :], hid_bank[s % 2][:, :], 0.0,
                                                   hid_hi[:, s % 2, :].bitcast(F32), ALU.max, ALU.subtract).then_inc(hid_split, 1)
                elif name == "gate":
                    wait(dve, gate_done, 1, j, 1)
                    nc.vector.tensor_scalar(gate_h[:, :, :], out_bank[0][:, 0:C].unsqueeze(2).to_broadcast([P, C, P]), 0.0, None,
                                            ALU.max).then_inc(gate_relu, 1)
                elif name == "logits":
                    wait(dve, logits_done, 1, j, 1)
                    linke(nc.vector.tensor_reduce(gate_s[:, 0:1], out_bank[1][:, 0:3], AX_X, ALU.max))
                    nc.vector.tensor_scalar(gate_s[:, 1:4], out_bank[1][:, 0:3], gate_s[:, 0:1], None, ALU.subtract
                                            ).then_inc(logits_read, 1)
                elif name == "mix":
                    wait(dve, gate_exp, 1, j, 1)
                    linke(nc.vector.tensor_reduce(gate_s[:, 7:8], gate_s[:, 4:7], AX_X, ALU.add))
                    linke(nc.vector.reciprocal(gate_s[:, 8:9], gate_s[:, 7:8]))
                    linke(nc.vector.tensor_scalar(gate_s[:, 9:12], gate_s[:, 4:7], gate_s[:, 8:9], None, ALU.mult))
                    y = e_out[:, CHOSEN, :, :]
                    linke(nc.vector.scalar_tensor_tensor(y, y, gate_s[:, 9:10], x3T[:, :, :], ALU.mult, ALU.add))
                    linke(nc.vector.scalar_tensor_tensor(y, e_out[:, 0, :, :], gate_s[:, 10:11], y, ALU.mult, ALU.add))
                    nc.vector.scalar_tensor_tensor(y, e_out[:, 1, :, :], gate_s[:, 11:12], y, ALU.mult, ALU.add).then_inc(mixed, 1)

            def turn(names, i, j):
                linked.clear()
                for name in own_order(names):
                    if name in REST:
                        rest(name, j)
                    else:
                        front(name, i)
                assert linked.get(front_link, FRONT_LINKS) == FRONT_LINKS, linked
                assert linked.get(rest_link, REST_LINKS) == REST_LINKS, linked

            dve.wait_ge(lin_in, 64)
            nc.vector.tensor_copy(lin_hi[:, :, :].rearrange("p n f -> p (n f)"), raw[:, :]).then_inc(consts_set, 1)
            dve.wait_ge(consts_set, 1)
            nc.vector.tensor_tensor(lin_lo[:, :, :].rearrange("p n f -> p (n f)"), raw[:, :],
                                    lin_hi[:, :, :].rearrange("p n f -> p (n f)").bitcast(F32), ALU.subtract).then_inc(lin_split, 1)
            dve.wait_ge(consts_in, 16 * 11)
            nc.vector.tensor_copy(lap_mats[:, :], e_out[:, 0, :, :].rearrange("p c t -> p (c t)")).then_inc(consts_set, 1)
            nc.vector.tensor_copy(len_f[:, :], len_sb[:, :]).then_inc(consts_set, 1)
            dve.wait_ge(consts_set, 3)
            nc.vector.tensor_scalar(mask_rows[:, :], iota_sb[:, :], len_f[:, :], MASKED, ALU.is_ge, ALU.mult).then_inc(mask_set, 1)
            dve.wait_ge(bias_done, 1)
            nc.vector.tensor_tensor(ebias[:, 0, :], pv_bank[0][:, 0:2], vec[:, :, BQ], ALU.add)
            nc.vector.tensor_tensor(ebias[:, 1, :], pv_bank[0][:, 3:6:2], vec[:, :, BK], ALU.add)
            nc.vector.tensor_tensor(ebias[:, 2, :], pv_bank[0][:, 2:6:2], vec[:, :, BK], ALU.add).then_inc(consts_set, 1)
            dve.wait_ge(consts_set, 4)
            turn(FRONT, 0, None)
            with dve.Fori(1, B) as i:
                turn(BOTH, i, i - 1)
            turn(REST, None, B - 1)

        @block.gpsimd
        def _(pool):
            def split_shared(n):
                pool.wait_ge(raw_in, 16 * (n + 1))
                cols = slice((n % 2) * C * F, (n % 2 + 1) * C * F)
                nc.gpsimd.tensor_copy(exp_hi[:, n // 2, cols], raw[:, :]).then_inc(w_hi_done, 1)
                pool.wait_ge(w_hi_done, n + 1)
                nc.gpsimd.tensor_tensor(exp_lo[:, n // 2, cols], raw[:, :], exp_hi[:, n // 2, cols].bitcast(F32),
                                        ALU.subtract).then_inc(w_split, 1)

            def split_chosen(n, j):
                wait(pool, chosen_hi, 2, j, n + 1)
                cols = slice(n * C * F, (n + 1) * C * F)
                nc.gpsimd.tensor_tensor(exp_lo[:, CHOSEN, cols], raw[:, :], exp_hi[:, CHOSEN, cols].bitcast(F32),
                                        ALU.subtract).then_inc(w_split, 1)

            def front(name, i, first):
                if name[0] == "S" and name != "S8" and name != "S12":
                    return
                if first and name in ("xT", "sT"):
                    split_shared(("xT", "sT").index(name))
                elif name == "kp" and not first:
                    split_chosen(0, i - 1)
                elif name == "S12" and not first:
                    split_chosen(1, i - 1)
                elif name == "vp":
                    wait(pool, v_hi, 1, i, 1)
                    for t in range(C):
                        v = v_prev[:, t, :].rearrange("p (h d) -> p h d", d=DH)
                        rest = v_rest[:, t, :].rearrange("p (h d) -> p h d", d=DH)
                        part = [v_cols[:, t, :, n * DH:(n + 1) * DH] for n in range(3)]
                        nc.gpsimd.tensor_tensor(part[1], v, part[0], ALU.subtract)
                        nc.gpsimd.tensor_tensor(rest, v, part[0], ALU.subtract).then_inc(v_link, 1)
                        wait(pool, v_link, C, i, t + 1)
                        last = nc.gpsimd.tensor_tensor(part[2], rest, part[1], ALU.subtract)
                    last.then_inc(v_split, 1)
                    if first:
                        split_shared(2)
                elif name == "S8" and first:
                    split_shared(3)
                elif name[0] == "E":
                    h = int(name[1:])
                    if h not in DVE_LO:
                        wait_freed_act(pool, i, name)
                        nc.gpsimd.tensor_tensor(prob_lo[:, h % NPROB, :], prob[:, h % NPROB, :], prob_hi[:, h % NPROB, :],
                                                ALU.subtract).then_inc(prob_split_pool, 1)

            nc.gpsimd.memset(q_rows[:, :, :].bitcast(F32), 1.0).then_inc(rows_set, 1)
            nc.gpsimd.memset(k_rows[:, :, :].bitcast(F32), 1.0).then_inc(rows_set, 1)
            nc.gpsimd.memset(v_cols[:, :, :, :], 1.0).then_inc(rows_set, 1)
            pool.wait_ge(rows_set, 3)
            for name in FRONT:
                front(name, 0, True)
            with pool.Fori(1, B) as i:
                for name in FRONT:
                    front(name, i, False)
            split_chosen(0, B - 1)
            split_chosen(1, B - 1)


def kernel(**inputs):
    import concourse.bacc as bacc
    from concourse.bass_utils import run_bass_kernel_spmd as run

    a = {k: np.ascontiguousarray(v) for k, v in inputs.items()}
    order = [8 * c + 4 * e + n for e in range(2) for n in range(4) for c in range(2)]
    v_perm = np.array([h * DH + d for h in order for d in range(DH)])
    qk_perm = np.array([P * c + 64 * e + DH * n + d for c in range(2) for e in range(2) for d in range(DH) for n in range(4)])
    wqkvo = np.stack([a["L2_cond_Wq"][:, qk_perm], a["L2_cond_Wk"][:, qk_perm], a["L2_cond_Wv"][:, v_perm],
                      a["L2_cond_Wo"][v_perm, :]])

    def by_partition(v):
        return v.reshape(C, P).T

    vecs = np.stack([by_partition(v) for v in (a["L2_cond_bq"][qk_perm], a["L2_cond_bk"][qk_perm], a["L2_cond_bo"],
                                               a["L2_cond_b_prev"].reshape(D), a["L2_cond_b_self"].reshape(D))], axis=2)
    lap = np.zeros((D, D), np.float32)
    for m in range(D):
        lap[m, m] = -2.0
        for k in (m - 1, m + 1):
            lap[k if 0 <= k < D else 2 * m - k, m] += 1.0
    ones = np.zeros((P, C, H), np.float32)
    for c in range(C):
        for m in range(P):
            ones[m, c, (m // 64) * HALF + 2 * (m % 4) + c] = 1.0
    consts = np.concatenate([np.eye(P, dtype=np.float32), lap[0:P, 0:P], lap[P:, P:], lap[P:, 0:P], lap[0:P, P:],
                             ones.reshape(P, C * H)], axis=1)
    iota = np.tile(np.arange(S, dtype=np.float32), (B, 1))

    arrays = {
        "x": a["x"], "side": a["fside_BxSxS_0"], "seq_len": a["itok_B_18_1004"].reshape(B, 1),
        "subject": a["itok_B_0_7"].reshape(1, B), "label": a["itok_B_0_2"].reshape(1, B),
        "z": np.stack([a["condB_zX"], a["condB_zY"], a["condB_zR"]], axis=1),
        "w0": a["L0_cond_weight"], "b0": a["L0_cond_bias"].reshape(-1, C, P).transpose(0, 2, 1),
        "wqkvo": wqkvo, "vecs": vecs, "bv": a["L2_cond_bv"][v_perm].reshape(1, D),
        "wi": a["L3_cond_wi"], "wo": a["L3_cond_wo"], "swi": a["L3_cond_swi"], "swo": a["L3_cond_swo"],
        "g1": a["L3_cond_g1"], "g2": a["L3_cond_g2"], "consts": consts, "iota": iota,
    }
    arrays = {f"in_{k}": np.ascontiguousarray(v) for k, v in arrays.items()}
    nc = bacc.Bacc("TRN2", target_bir_lowering=False, num_devices=1, dynamic_dma_scratch_size=1024)
    args = [nc.dram_tensor(k, v.shape, mybir.dt.from_np(v.dtype), kind="ExternalInput").ap() for k, v in arrays.items()]
    out = nc.dram_tensor("out", (B, S, D), F32, kind="ExternalOutput").ap()
    build(nc, *args, out)
    return run(nc, [arrays], core_ids=[0]).results[0]["out"]
```

```python
from contextlib import ExitStack

import numpy as np

import concourse.bass as bass
from concourse import mybir

ALU = mybir.AluOpType
ACT = mybir.ActivationFunctionType
F32 = mybir.dt.float32
F32R = mybir.dt.float32r
BF16 = mybir.dt.bfloat16
F16 = mybir.dt.float16
I32 = mybir.dt.int32
AX_X = mybir.AxisListType.X

P = 128
B = 16
S = 256
D = 256
C = D // P
H = 16
DH = D // H
SCALE = 1.0 / DH ** 0.5
HALF = H // 2
F = 1024
FC = F // P
NE = 3
CHOSEN = 2
STEPS = 4
LSTEPS = NE * STEPS
VW = 3 * DH + 1
ROWS_MAX = 3 * DH + 1
ROWS_EXP = ROWS_MAX + 2
MASKED = -1.0e30

EARLY = ["x1", "ks", "q", "lap", "vs"]
ATTENTION = (["kp", "vp"] + [f"S{h}" for h in range(H)] + ["mT"] + [f"E{h}" for h in range(H)])
USES = EARLY + ATTENTION
USE = {name: n for n, name in enumerate(USES)}
NU = len(USES)
assert NU % 2 == 0
ACT_FREES = {"ks", "q", "vs"} | {f"E{h}" for h in range(H)}
ACT_ORDER = [x for x in USES if x in ACT_FREES]
DVE_ORDER = [x for x in USES if x not in ACT_FREES]
HI_OF = {name: n + 1 for n, name in enumerate(["q", "kp"])}
NHI = len(HI_OF)

STEP = [("S7", "H4 x_parts"), ("S8", "w_parts"), ("S9", "P3"), ("S10", "s_parts"), ("S11", "H5 wo_part0"),
        ("S13", "P4 wo_part1"), ("S15", "H6 wo_part2"), ("mT", "P5 H7 P6 gate0 wo_part3"), ("E1", "H8"),
        ("E2", "P7"), ("E4", "H9"), ("E6", "P8"), ("E10", "half H10"), ("E12", "norm P9 gate1"), ("E14", "H11"),
        ("E15", "P10 pvend att"), ("x1", "P11 gate2 x1_parts"), ("ks", "aT gate relu react"), ("q", "logits"),
        ("lap", "mix x2_parts scale wo"), ("vs", "x3_parts"), ("vp", "sum H0 self H1 P0 H2"), ("S1", "P1 wi_part"),
        ("S3", "H3 store wo_load"), ("S5", "P2")]
FIRST_HALF = ATTENTION.index("S5") + 1
DVE_LATER = {"H2": "S1", "H3": "S5", "H4": "S9", "H5": "S13", "H6": "mT", "aT": "relu"}
AFTER = {name: rest.split() for name, rest in STEP}
FRONT = ATTENTION[FIRST_HALF:] + EARLY + ATTENTION[:FIRST_HALF]
BODY = [x for stage in FRONT for x in [stage] + AFTER.get(stage, [])]
DVE_BODY = list(BODY)
for name, later in DVE_LATER.items():
    DVE_BODY.remove(name)
    DVE_BODY.insert(DVE_BODY.index(later) + 1, name)
LAGS = (EARLY + ATTENTION[:FIRST_HALF] + ["x_parts", "w_parts", "s_parts", "x1_parts", "x2_parts", "react", "self"],
        ATTENTION[FIRST_HALF:] + ["half", "norm", "pvend", "att", "aT", "wo", "x3_parts"]
        + [x for stage in ATTENTION[:FIRST_HALF] for x in AFTER.get(stage, []) if x not in ("sum", "self", "store")])
LAG = {x: 0 if x in LAGS[0] else 1 if x in LAGS[1] else 2 for x in BODY}
SHARED_AT = ["vs", "kp", "vp", "S1", "S4", "S7", "S10", "S13"]
SHARED = len(SHARED_AT)
LIN_ORDER = [1, 0, 2, 3]
PARTS = 5
FIRST, LAST = 2, B


def in_turn(i, names=BODY):
    for name in names:
        if not isinstance(i, int) or 0 <= i - LAG[name] < B:
            yield name, i - LAG[name]


NPROB = 3
BEHIND = 3
DVE_PARTS = [h for h in range(H) if h % 2]
N_LO_DVE = [sum(g in DVE_PARTS for g in range(h + 1)) for h in range(H)]
N_LO_POOL = [h + 1 - N_LO_DVE[h] for h in range(H)]

BQ, BK, BO, BV, B_PREV, B_SELF, NVEC = range(7)
LINKS = {"early": 3, "attention": 3 + H // 2, "rest": NE * C + 2}


def wait(eng, sem, per_turn, turn, n):
    value = turn * per_turn + n
    if isinstance(value, int) and value <= 0:
        return
    eng.wait_ge(sem, value)


def build(nc, x, side, seq_len, subject, label, z, w0, b0, wqkvo, vecs, wi, wo, swi, swo,
          g1, g2, consts, iota, out):
    with ExitStack() as ctx:
        def sb(name, shape, dt=F32):
            return ctx.enter_context(nc.sbuf_tensor(name, shape, dt))

        def bank(name):
            return ctx.enter_context(nc.psum_tensor(name, [P, 512], F32))

        def sem(name):
            return ctx.enter_context(nc.semaphore(name))

        exp_hi = sb("exp_hi", [P, NE, 2 * C * F], F32R)
        exp_lo = sb("exp_lo", [P, NE, 2 * C * F], F32R)
        raw = sb("raw", [P, C * F])
        lin_hi = sb("lin_hi", [P, 4, C * D], F32R)
        lin_lo = sb("lin_lo", [P, 4, C * D], F32R)
        gate1 = sb("gate1", [P, NE * C, D])
        gate2 = sb("gate2", [P, C, 3])
        ident = sb("ident", [P, P])
        head_ones = sb("head_ones", [P, C * H])
        lap_mats = sb("lap_mats", [P, 4 * P], F32R)
        vec = sb("vec", [P, C, NVEC])
        ebias = sb("ebias", [P, 3, C])
        len_sb = sb("len_sb", [B, 1], I32)
        len_f = sb("len_f", [B, 1])
        subject_sb = sb("subject_sb", [1, B], I32)
        label_sb = sb("label_sb", [1, B], I32)

        x_raw = sb("x_raw", [P, C, S])
        s_raw = sb("s_raw", [P, C, S])
        w0_raw = sb("w0_raw", [P, C, D])
        b0_sb = sb("b0_sb", [P, C])
        z_sb = sb("z_sb", [P, 3])
        z_neg = sb("z_neg", [P, 1])
        z_mid = sb("z_mid", [P, 1])
        x1T = sb("x1T", [P, C, S])
        att = sb("att", [P, C, D])
        ak_hi = sb("ak_hi", [P, C, S], F32R)
        ak_lo = sb("ak_lo", [P, C, S], F32R)
        x_hi = sb("x_hi", [P, C, S], F32R)
        x_lo = sb("x_lo", [P, C, S], F32R)
        s_hi = sb("s_hi", [P, C, S], F32R)
        s_lo = sb("s_lo", [P, C, S], F32R)
        p_hi = sb("p_hi", [P, C, S], F32R)
        p_lo = sb("p_lo", [P, C, S], F32R)
        ksT = sb("ksT", [P, C, S])
        react = sb("react", [P, C, S])
        beside = sb("beside", [P, C, S])
        v_rest = beside
        q_full = sb("q_full", [P, C, S])
        x2b = sb("x2b", [P, C, S])
        x3T = sb("x3T", [P, C, S])
        x3_hi = sb("x3_hi", [P, C, S], F32R)
        x3_lo = sb("x3_lo", [P, C, S], F32R)
        q_rows = sb("q_rows", [P, HALF, S], F32R)
        k_rows = sb("k_rows", [P, HALF, S], F32R)
        v_self = sb("v_self", [P, C, D])
        v_cols = sb("v_cols", [P, C, H, VW], BF16)
        s_self = sb("s_self", [P, C, H])
        s_max = sb("s_max", [P, C, H])
        d_self = sb("d_self", [P, C, H])
        p_self = sb("p_self", [P, C, H])
        max_rows = sb("max_rows", [H, 2, S], F32R)
        mask_rows = max_rows[0:B, 0, :]
        prob = sb("prob", [P, NPROB, 2 * S])
        prob_hi = sb("prob_hi", [P, NPROB, 2 * S], F16)
        prob_lo = sb("prob_lo", [P, NPROB, 2 * S], F16)
        den = sb("den", [P, C, H])

        hid_hi = sb("hid_hi", [P, 2, 2 * S], F32R)
        hid_lo = sb("hid_lo", [P, 2, 2 * S], F32R)
        e_out = sb("e_out", [P, NE, C, S])
        gate_h = sb("gate_h", [P, C, P])
        gate_s = sb("gate_s", [P, 12])
        gate_terms = sb("gate_terms", [P, D])
        iota_sb = gate_terms[0:B, :]
        ones = sb("ones", [P, 1])

        mask_dram = nc.dram_tensor("mask_scratch", (B, S), F32R, kind="Internal").ap()

        front_bank = [bank("front0"), bank("front1")]
        pv_bank = [bank("pv0"), bank("pv1")]
        hid_bank = [bank("hid0"), bank("hid1")]
        out_bank = [bank("out0"), bank("out1")]

        choice_in = sem("choice_in")
        consts_in = sem("consts_in")
        gate_in = sem("gate_in")
        lin_in = sem("lin_in")
        consts_set = sem("consts_set")
        bias_done = sem("bias_done")
        mask_set = sem("mask_set")
        rows_set = sem("rows_set")
        lin_hi_done = sem("lin_hi_done")
        lin_split = sem("lin_split")
        x_in = sem("x_in")
        s_in = sem("s_in")
        w0_in = sem("w0_in")
        small_in = sem("small_in")
        raw_in = sem("raw_in")
        shared_in = [sem("shared_even_in"), sem("shared_odd_in")]
        filled = sem("filled")
        freed_act = sem("freed_act")
        freed_dve = sem("freed_dve")
        hi_done = sem("hi_done")
        in_hi = sem("in_hi")
        in_split = sem("in_split")
        self_done = sem("self_done")
        x1_split = sem("x1_split")
        beside_done = sem("beside_done")
        react_done = sem("react_done")
        x1_hi = sem("x1_hi")
        x2_hi = sem("x2_hi")
        q_split = sem("q_split")
        qk_done = sem("qk_done")
        x2_split = sem("x2_split")
        x3_done = sem("x3_done")
        x3_hi_done = sem("x3_hi_done")
        x3_split = sem("x3_split")
        q_placed = sem("q_placed")
        k_placed = sem("k_placed")
        mask_placed = sem("mask_placed")
        max_placed = sem("max_placed")
        v_hi = sem("v_hi")
        v_split = sem("v_split")
        max_done = sem("max_done")
        d_self_done = sem("d_self_done")
        p_self_done = sem("p_self_done")
        prob_split_dve = sem("prob_split_dve")
        prob_split_pool = sem("prob_split_pool")
        pv_done = sem("pv_done")
        pv_freed = sem("pv_freed")
        own_done = sem("own_done")
        att_done = sem("att_done")
        att_turned = sem("att_turned")
        att_hi_done = sem("att_hi_done")
        att_split = sem("att_split")
        wo_done = sem("wo_done")
        shared_hi = sem("shared_hi")
        w_split = sem("w_split")
        chosen_hi = sem("chosen_hi")
        hid_filled = sem("hid_filled")
        hid_hi_done = sem("hid_hi_done")
        hid_split = sem("hid_split")
        step_done = sem("step_done")
        e_out_done = sem("e_out_done")
        gate_terms_done = sem("gate_terms_done")
        gate_done = sem("gate_done")
        gate_relu = sem("gate_relu")
        logits_done = sem("logits_done")
        logits_read = sem("logits_read")
        gate_exp = sem("gate_exp")
        gate_set = sem("gate_set")
        scaled = sem("scaled")
        chosen_added = sem("chosen_added")
        mix_link = sem("mix_link")
        mixed = sem("mixed")
        stored = sem("stored")
        early_link = sem("early_link")
        attention_link = sem("attention_link")
        rest_link = sem("rest_link")

        def front_psum(name):
            return front_bank[USE[name] % 2]

        def chunked(t):
            return t[:, :].rearrange("p (c t) -> p c t", c=C)

        def wait_filled(eng, i, name):
            wait(eng, filled, NU, i, USE[name] + 1)

        def wait_freed_dve(eng, i, name):
            wait(eng, freed_dve, len(DVE_ORDER), i, DVE_ORDER.index(name) + 1)

        def wait_freed_act(eng, i, name):
            wait(eng, freed_act, len(ACT_ORDER), i, ACT_ORDER.index(name) + 1)

        def wait_prob_split(eng, i, h):
            if h in DVE_PARTS:
                wait(eng, prob_split_dve, N_LO_DVE[-1], i, N_LO_DVE[h])
            elif h >= 0:
                wait(eng, prob_split_pool, N_LO_POOL[-1], i, N_LO_POOL[h])

        def shared_piece(n):
            size = C * F // 2
            return slice(n % 4 * size, (n % 4 + 1) * size), slice(n % 2 * size, (n % 2 + 1) * size)

        def expert_w(part, e):
            w_in = part[:, e, 0:C * F].rearrange("p (k f) -> p k f", k=C)
            w_out = part[:, e, C * F:2 * C * F].rearrange("p (f d) -> p f d", d=D)
            return w_in, w_out

        block = ctx.enter_context(nc.Block())

        @block.sync
        def _(sp):
            def load_x(b):
                sp.dma_start(x_raw[:, :, :], x[bass.ds(b, 1)].rearrange("o (c p) t -> p (o c) t", p=P)).then_inc(x_in, 16)

            def load_s(b):
                sp.dma_start(s_raw[:, :, :], side[bass.ds(b, 1)].rearrange("o (c p) t -> p (o c) t", p=P)).then_inc(s_in, 16)

            def chooser(row, b, count):
                return sp.value_load(row[0:1, bass.ds(b, 1)], min_val=0, max_val=count - 1)

            def load_w0(who):
                sp.dma_start(w0_raw[:, :, :], w0[bass.ds(who, 1)].rearrange("o (k p) f -> p (o k) f", p=P)).then_inc(w0_in, 16)

            def load_small(b, who):
                sp.dma_start(b0_sb[:, :], b0[bass.ds(who, 1)].rearrange("o p c -> (o p) c")).then_inc(small_in, 16)
                sp.dma_start(z_sb[:, :], z[bass.ds(b, 1)].to_broadcast([P, 3])).then_inc(small_in, 16)

            def load_wi(kind):
                sp.dma_start(raw[:, :].rearrange("p (k f) -> p k f", k=C),
                             wi[bass.ds(kind, 1)].rearrange("o (k p) f -> p (o k) f", p=P)).then_inc(raw_in, 16)

            def load_wo(kind):
                sp.dma_start(raw[:, :].rearrange("p (f d) -> p f d", d=D),
                             wo[bass.ds(kind, 1)].rearrange("o (f p) d -> p (o f) d", p=P)).then_inc(raw_in, 16)

            def load_shared(n):
                e, half, (_, at) = n // 4, n % 2, shared_piece(n)
                if n % 4 < 2:
                    sp.dma_start(raw[:, at], swi[e, half * P:(half + 1) * P]).then_inc(shared_in[half], 16)
                else:
                    chunks = F // 2
                    sp.dma_start(raw[:, at].rearrange("p (f d) -> p f d", d=D),
                                 swo[e, half * chunks:(half + 1) * chunks].rearrange("(f p) d -> p f d", p=P)).then_inc(shared_in[half], 16)

            def place(rows, part, first_row, done):
                for e in range(2):
                    sp.dma_start(rows[64 * e + first_row:64 * e + first_row + DH, :, :].bitcast(F32),
                                 part[64 * e:64 * e + 64, :, :].bitcast(F32)).then_inc(done, 16)

            def stage(name, i):
                if name == "x1":
                    who = chooser(subject_sb, (i + 1) % B, w0.shape[0])
                    wait_freed_dve(sp, i, "x1")
                    load_x((i + 1) % B)
                    sp.dma_start(k_rows[3 * DH:64 + 3 * DH + 1:64, :, :].bitcast(F32),
                                 mask_dram[bass.ds(i, 1), :].bitcast(F32).unsqueeze(1).to_broadcast([2, HALF, S])
                                 ).then_inc(mask_placed, 16)
                    wait(sp, in_split, 3, i, 3)
                    load_w0(who)
                    load_s((i + 1) % B)
                elif name == "q":
                    wait(sp, hi_done, NHI, i, HI_OF["q"])
                    place(q_rows, p_hi, 0, q_placed)
                    place(q_rows, p_hi, 2 * DH, q_placed)
                elif name == "lap":
                    wait(sp, q_split, 1, i, 1)
                    place(q_rows, p_lo, DH, q_placed)
                elif name == "kp":
                    wait(sp, hi_done, NHI, i, HI_OF["kp"])
                    place(k_rows, ak_hi, 0, k_placed)
                    place(k_rows, ak_hi, DH, k_placed)
                    wait_freed_dve(sp, i, "kp")
                    place(k_rows, ak_lo, 2 * DH, k_placed)
                elif name == "self":
                    who = chooser(subject_sb, (i + 1) % B, w0.shape[0])
                    wait(sp, x2_split, 1, i, 1)
                    load_small((i + 1) % B, who)
                elif name == "mT":
                    wait_freed_dve(sp, i, "mT")
                    for j in range(2):
                        row = ROWS_MAX + j
                        sp.dma_start(q_rows[row:64 + row + 1:64, :, :].bitcast(F32),
                                     max_rows[:, j, :].bitcast(F32)).then_inc(max_placed, 16)
                elif name == "E12":
                    kind = chooser(label_sb, i, wi.shape[0])
                    wait(sp, w_split, PARTS, i, SHARED)
                    load_wi(kind)
                elif name == "wo_load":
                    kind = chooser(label_sb, i, wo.shape[0])
                    wait(sp, w_split, PARTS, i, SHARED + 1)
                    load_wo(kind)
                elif name == "store":
                    wait(sp, mixed, 1, i, 1)
                    sp.dma_start(out[bass.ds(i, 1)].rearrange("o (c p) t -> p (o c) t", p=P), e_out[:, CHOSEN, :, :]).then_inc(stored, 16)

            sp.dma_start(subject_sb[:, :], subject).then_inc(choice_in, 16)
            load_x(0)
            sp.wait_ge(choice_in, 16)
            load_w0(chooser(subject_sb, 0, w0.shape[0]))
            load_small(0, chooser(subject_sb, 0, w0.shape[0]))
            load_s(0)
            sp.dma_start(vec[:, :, :], vecs).then_inc(consts_in, 16)
            for n in LIN_ORDER:
                sp.dma_start(raw[:, n * C * D:(n + 1) * C * D].rearrange("p (k f) -> p k f", k=C),
                             wqkvo[n].rearrange("(k p) f -> p k f", p=P)).then_inc(lin_in, 16)
            sp.dma_start(e_out[:, 0, :, :].rearrange("p c t -> p (c t)"), consts[:, P:5 * P]).then_inc(consts_in, 16)
            sp.dma_start(ident[:, :], consts[:, 0:P]).then_inc(consts_in, 16)
            sp.dma_start(iota_sb, iota).then_inc(consts_in, 16)
            sp.dma_start(len_sb[:, :], seq_len).then_inc(consts_in, 16)
            sp.dma_start(head_ones[:, :], consts[:, 5 * P:5 * P + C * H]).then_inc(consts_in, 16)
            sp.dma_start(label_sb[:, :], label).then_inc(choice_in, 16)
            sp.wait_ge(mask_set, 1)
            sp.dma_start(mask_dram.bitcast(F32), mask_rows.bitcast(F32)).then_inc(stored, 16)
            sp.wait_ge(bias_done, 1)
            sp.wait_ge(lin_split, 2)
            load_shared(0)
            sp.wait_ge(lin_split, 4)
            load_shared(1)
            sp.dma_start(gate1[:, :, :], g1.rearrange("(k p) f -> p k f", p=P)).then_inc(gate_in, 16)
            sp.dma_start(gate2[:, :, :], g2.rearrange("(k p) f -> p k f", p=P)).then_inc(gate_in, 16)
            sp.wait_ge(choice_in, 32)
            sp.wait_ge(stored, 16)
            sp.wait_ge(rows_set, 2)
            for i in range(FIRST):
                for name, seq in in_turn(i):
                    stage(name, seq)
                    if seq == 0 and name in SHARED_AT[1:-1]:
                        n = SHARED_AT.index(name) + 1
                        sp.wait_ge(w_split, n - 1)
                        load_shared(n)
            with sp.Fori(FIRST, LAST) as i:
                for name, seq in in_turn(i):
                    stage(name, seq)
            for i in range(LAST, B + 2):
                for name, seq in in_turn(i):
                    stage(name, seq)
            sp.wait_ge(x_in, 16 * (B + 1))
            sp.wait_ge(s_in, 16 * (B + 1))
            sp.wait_ge(w0_in, 16 * (B + 1))
            sp.wait_ge(small_in, 32 * (B + 1))
            sp.wait_ge(stored, 16 * (B + 1))

        @block.tensor
        def _(pe):
            def product(acc, w_hi, w_lo, a_hi, a_lo, first, last):
                nc.tensor.matmul(acc, w_hi, a_hi, start=first, stop=False)
                nc.tensor.matmul(acc, w_hi, a_lo, start=False, stop=False)
                return nc.tensor.matmul(acc, w_lo, a_hi, start=False, stop=last)

            def linear(n):
                return (lin_hi[:, n, :].rearrange("p (k f) -> p k f", k=C),
                        lin_lo[:, n, :].rearrange("p (k f) -> p k f", k=C))

            def feature_major(psum, w, a_hi, a_lo):
                for c in range(C):
                    for k in range(C):
                        last = product(psum[:, c * S:(c + 1) * S], w[0][:, k, c * P:(c + 1) * P],
                                       w[1][:, k, c * P:(c + 1) * P], a_hi[:, k, :], a_lo[:, k, :], k == 0, k == C - 1)
                return last

            def token_major(psum, w, a_hi, a_lo):
                for t in range(C):
                    for k in range(C):
                        last = product(psum[:, t * D:(t + 1) * D], a_hi[:, k, t * P:(t + 1) * P],
                                       a_lo[:, k, t * P:(t + 1) * P], w[0][:, k, :], w[1][:, k, :], k == 0, k == C - 1)
                return last

            def transposed(psum, src):
                for c in range(C):
                    for t in range(C):
                        last = nc.tensor.transpose(psum[:, c * S + t * P:c * S + (t + 1) * P],
                                                   src[:, t, c * P:(c + 1) * P], ident[:, :])
                return last

            def open_bank(i, name):
                u, seq = USE[name] - 2, i
                if u < 0:
                    u, seq = u + NU, i - 1
                (wait_freed_act if USES[u] in ACT_FREES else wait_freed_dve)(pe, seq, USES[u])
                return front_bank[USE[name] % 2]

            def attend(i, h):
                wait_prob_split(pe, i, h)
                if h == 0:
                    wait(pe, v_split, 1, i, 1)
                for t in range(C):
                    if h == HALF:
                        wait(pe, pv_freed, 2 * C, i, t + 1)
                    acc = pv_bank[t][:, (h % HALF) * VW:(h % HALF + 1) * VW]
                    for k in range(C):
                        at = k * S + t * P
                        nc.tensor.matmul(acc, prob_hi[:, h % NPROB, at:at + P], v_cols[:, k, h, :], start=(k == 0), stop=False)
                        last = nc.tensor.matmul(acc, prob_lo[:, h % NPROB, at:at + P], v_cols[:, k, h, :],
                                                start=False, stop=(k == C - 1))
                last.then_inc(pv_done, 1)

            def front(name, i):
                if name == "self":
                    wait(pe, qk_done, 1, i, 1)
                    for t in range(C):
                        for c in range(C):
                            last = nc.tensor.matmul(pv_bank[0][:, t * H:(t + 1) * H], ksT[:, c, t * P:(t + 1) * P],
                                                    head_ones[:, c * H:(c + 1) * H], start=(c == 0), stop=(c == C - 1))
                    last.then_inc(self_done, 1)
                    return
                if name == "pvend":
                    for h in range(H - BEHIND, H):
                        attend(i, h)
                    return
                psum = open_bank(i, name)
                if name == "x1":
                    wait(pe, in_split, 3, i, 2)
                    last = feature_major(psum, (p_hi, p_lo), x_hi, x_lo)
                elif name == "ks":
                    wait(pe, in_split, 3, i, 3)
                    last = feature_major(psum, linear(1), s_hi, s_lo)
                elif name == "q":
                    last = feature_major(psum, linear(0), s_hi, s_lo)
                elif name == "lap":
                    wait(pe, x1_split, 1, i, 1)
                    for c in range(C):
                        acc = psum[:, c * S:(c + 1) * S]
                        own = lap_mats[:, c * P:(c + 1) * P]
                        across = lap_mats[:, (2 + c) * P:(3 + c) * P]
                        nc.tensor.matmul(acc, own, x_hi[:, c, :], start=True, stop=False)
                        nc.tensor.matmul(acc, own, x_lo[:, c, :], start=False, stop=False)
                        nc.tensor.matmul(acc, across, x_hi[:, 1 - c, :], start=False, stop=False)
                        last = nc.tensor.matmul(acc, across, x_lo[:, 1 - c, :], start=False, stop=True)
                elif name == "vs":
                    last = token_major(psum, linear(2), s_hi, s_lo)
                elif name == "kp":
                    wait(pe, x2_split, 1, i, 1)
                    last = feature_major(psum, linear(1), x_hi, x_lo)
                elif name == "vp":
                    last = token_major(psum, linear(2), x_hi, x_lo)
                elif name[0] == "S":
                    h = int(name[1:])
                    if h == 0:
                        wait(pe, q_placed, 16 * 6, i, 16 * 6)
                        wait(pe, k_placed, 16 * 6, i, 16 * 6)
                        wait(pe, mask_placed, 16, i, 16)
                    at, slot = 64 * (h // HALF), h % HALF
                    for t in range(C):
                        last = nc.tensor.matmul(psum[:, t * S:(t + 1) * S], q_rows[at:at + ROWS_MAX, slot, t * P:(t + 1) * P],
                                                k_rows[at:at + ROWS_MAX, slot, :], start=True, stop=True)
                elif name == "mT":
                    wait(pe, max_done, 1, i, 1)
                    for t in range(C):
                        last = nc.tensor.transpose(psum[0:H, t * P:(t + 1) * P], s_max[:, t, :], ident[:, :])
                elif name[0] == "E":
                    h = int(name[1:])
                    if h == 0:
                        wait(pe, max_placed, 16 * 2, i, 16 * 2)
                    at, slot = 64 * (h // HALF), h % HALF
                    for k in range(C):
                        last = nc.tensor.matmul(psum[:, k * S:(k + 1) * S], k_rows[at:at + ROWS_EXP, slot, k * P:(k + 1) * P],
                                                q_rows[at:at + ROWS_EXP, slot, :], start=True, stop=True)
                last.then_inc(filled, 1)
                if name[0] == "E" and int(name[1:]) >= BEHIND:
                    attend(i, int(name[1:]) - BEHIND)

            def hidden(s, j):
                e = s // STEPS
                (hi, _), (lo, _) = expert_w(exp_hi, e), expert_w(exp_lo, e)
                if s == 0:
                    wait(pe, x3_split, 1, j, 1)
                    pe.wait_ge(w_split, SHARED)
                    pe.wait_ge(gate_in, 32)
                    pe.wait_ge(rows_set, 4)
                if s == CHOSEN * STEPS:
                    wait(pe, w_split, PARTS, j, SHARED + 1)
                if s >= 2:
                    wait(pe, hid_split, LSTEPS, j, s - 1)
                psum = hid_bank[s % 2]
                for f in range(2):
                    at = (2 * (s % STEPS) + f) * P
                    for k in range(C):
                        last = product(psum[:, f * S:(f + 1) * S], hi[:, k, at:at + P], lo[:, k, at:at + P],
                                       x3_hi[:, k, :], x3_lo[:, k, :], k == 0, k == C - 1)
                last.then_inc(hid_filled, 1)

            def project(s, j):
                e = s // STEPS
                (_, hi), (_, lo) = expert_w(exp_hi, e), expert_w(exp_lo, e)
                wait(pe, hid_split, LSTEPS, j, s + 1)
                if s and s % STEPS == 0:
                    wait(pe, e_out_done, NE, j, e)
                for f in range(2):
                    n = 2 * (s % STEPS) + f
                    if e == CHOSEN and f == 0:
                        wait(pe, w_split, PARTS, j, SHARED + 2 + s % STEPS)
                    for c in range(C):
                        last = product(out_bank[c][:, 0:S], hi[:, n, c * P:(c + 1) * P], lo[:, n, c * P:(c + 1) * P],
                                       hid_hi[:, s % 2, f * S:(f + 1) * S], hid_lo[:, s % 2, f * S:(f + 1) * S],
                                       n == 0, n == FC - 1)
                last.then_inc(step_done, 1)

            def rest(name, j):
                if name == "aT":
                    wait(pe, att_done, 1, j, 1)
                    transposed(pv_bank[0], att).then_inc(att_turned, 1)
                elif name == "wo":
                    wait(pe, att_split, 1, j, 1)
                    feature_major(pv_bank[1], linear(3), ak_hi, ak_lo).then_inc(wo_done, 1)
                elif name[0] == "H":
                    hidden(int(name[1:]), j)
                elif name[0] == "P":
                    project(int(name[1:]), j)
                elif name == "gate":
                    wait(pe, gate_terms_done, 1, j, 1)
                    for c in range(C):
                        last = nc.tensor.matmul(out_bank[c][:, S:S + 1], gate_terms[:, c * P:(c + 1) * P], ones[:, :], start=True, stop=True)
                    last.then_inc(gate_done, 1)
                elif name == "logits":
                    wait(pe, gate_relu, 1, j, 1)
                    for c in range(C):
                        last = nc.tensor.matmul(out_bank[0][:, 0:3], gate_h[:, c, :], gate2[:, c, :],
                                                start=(c == 0), stop=(c == C - 1))
                    last.then_inc(logits_done, 1)

            def bias_products():
                pe.wait_ge(lin_in, 64)
                pe.wait_ge(consts_in, 16 * 6)
                for c in range(C):
                    for k in range(C):
                        at = k * D + c * P
                        nc.tensor.matmul(pv_bank[0][:, c:c + 1], raw[:, at:at + P], vec[:, k, B_SELF:B_SELF + 1],
                                         start=(k == 0), stop=(k == C - 1))
                for c in range(C):
                    for k in range(C):
                        at = C * D + k * D + c * P
                        last = nc.tensor.matmul(pv_bank[0][:, 2 + 2 * c:4 + 2 * c], raw[:, at:at + P],
                                                vec[:, k, B_PREV:B_PREV + 2], start=(k == 0), stop=(k == C - 1))
                last.then_inc(bias_done, 1)

            def setup_before(name):
                if name == "ks":
                    bias_products()
                    pe.wait_ge(lin_split, 1)
                elif name == "q":
                    pe.wait_ge(lin_split, 2)
                elif name == "lap":
                    pe.wait_ge(consts_set, 1)
                elif name == "vs":
                    pe.wait_ge(lin_split, 4)

            def stage(name, seq):
                if name in USE or name in ("pvend", "self"):
                    front(name, seq)
                else:
                    rest(name, seq)

            for i in range(FIRST):
                for name, seq in in_turn(i):
                    if seq == 0:
                        setup_before(name)
                    stage(name, seq)
            with pe.Fori(FIRST, LAST) as i:
                for name, seq in in_turn(i):
                    stage(name, seq)
            for i in range(LAST, B + 2):
                for name, seq in in_turn(i):
                    stage(name, seq)

        @block.scalar
        def _(act):
            def round_hi(i, name, dst, bias=None):
                wait_filled(act, i, name)
                psum = chunked(front_psum(name))
                if bias is None:
                    last = nc.scalar.activation(dst[:, :, :], psum, ACT.Copy)
                else:
                    for c in range(C):
                        last = nc.scalar.activation(dst[:, c, :], psum[:, c, :], ACT.Identity, bias=bias[:, c:c + 1])
                last.then_inc(hi_done, 1)

            def front(name, i):
                if name == "x_parts":
                    wait(act, x_in, 16, i, 16)
                    nc.scalar.activation(x_hi[:, :, :], x_raw[:, :, :], ACT.Copy).then_inc(in_hi, 1)
                elif name == "w_parts":
                    wait(act, w0_in, 16, i, 16)
                    wait(act, q_placed, 16 * 6, i, 0)
                    nc.scalar.activation(p_hi[:, :, :], w0_raw[:, :, :], ACT.Copy).then_inc(in_hi, 1)
                elif name == "s_parts":
                    wait(act, s_in, 16, i, 16)
                    nc.scalar.activation(s_hi[:, :, :], s_raw[:, :, :], ACT.Copy).then_inc(in_hi, 1)
                elif name == "react":
                    wait_freed_dve(act, i, "x1")
                    nc.scalar.activation(react[:, :, :], x1T[:, :, :], ACT.Identity, bias=z_mid[:, :], scale=z_neg[:, :]
                                         ).then_inc(react_done, 1)
                elif name == "ks":
                    wait_filled(act, i, name)
                    psum = chunked(front_psum(name))
                    for c in range(C):
                        last = nc.scalar.activation(ksT[:, c, :], psum[:, c, :], ACT.Identity, bias=ebias[:, 1, c:c + 1])
                    last.then_inc(freed_act, 1)
                elif name == "q":
                    wait_filled(act, i, name)
                    wait(act, qk_done, 1, i - 1, 1)
                    psum = chunked(front_psum(name))
                    for c in range(C):
                        last = nc.scalar.activation(q_full[:, c, :], psum[:, c, :], ACT.Identity, bias=ebias[:, 0, c:c + 1])
                    last.then_inc(freed_act, 1)
                    wait_freed_act(act, i, name)
                    nc.scalar.activation(p_hi[:, :, :], q_full[:, :, :], ACT.Copy).then_inc(hi_done, 1)
                elif name == "x1_parts":
                    wait_freed_dve(act, i, "x1")
                    nc.scalar.activation(x_hi[:, :, :], x1T[:, :, :], ACT.Copy).then_inc(x1_hi, 1)
                elif name == "x2_parts":
                    wait_freed_dve(act, i, "lap")
                    nc.scalar.activation(x_hi[:, :, :], react[:, :, :], ACT.Copy).then_inc(x2_hi, 1)
                elif name == "kp":
                    round_hi(i, name, ak_hi, ebias[:, 2, :])
                elif name == "vs":
                    wait_filled(act, i, name)
                    nc.scalar.activation(v_self[:, :, :], chunked(front_psum(name)), ACT.Copy).then_inc(freed_act, 1)
                elif name == "vp":
                    wait_filled(act, i, name)
                    psum = chunked(front_psum(name))
                    for t in range(C):
                        last = nc.scalar.activation(v_cols[:, t, :, 0:DH], psum[:, t, :].rearrange("p (h d) -> p h d", d=DH), ACT.Copy)
                    last.then_inc(v_hi, 1)
                elif name == "mT":
                    wait(act, d_self_done, 1, i, 1)
                    nc.scalar.activation(p_self[:, :, :], d_self[:, :, :], ACT.Exp, scale=SCALE).then_inc(p_self_done, 1)
                elif name[0] == "E":
                    h = int(name[1:])
                    wait_filled(act, i, name)
                    if h >= NPROB:
                        wait_prob_split(act, i, h - NPROB)
                    psum = front_psum(name)
                    last = nc.scalar.activation(prob[:, h % NPROB, :], psum[:, :], ACT.Exp, scale=SCALE)
                    if h not in DVE_PARTS:
                        if h >= NPROB:
                            wait(act, pv_done, H, i, h - NPROB + 1)
                        last = nc.scalar.activation(prob_hi[:, h % NPROB, :], psum[:, :], ACT.Exp, scale=SCALE)
                    last.then_inc(freed_act, 1)

            def shared_hi_part(n):
                to, at = shared_piece(n)
                act.wait_ge(shared_in[n % 2], 16 * (n // 2 + 1))
                nc.scalar.activation(exp_hi[:, n // 4, to], raw[:, at], ACT.Copy).then_inc(shared_hi, 1)

            def chosen_hi_part(first, last, loaded, j):
                wait(act, raw_in, 32, j, 16 * loaded)
                at = first % (C * F)
                nc.scalar.activation(exp_hi[:, CHOSEN, first:last], raw[:, at:at + last - first], ACT.Copy).then_inc(chosen_hi, 1)

            def keep_output(e, j):
                wait(act, step_done, LSTEPS, j, (e + 1) * STEPS)
                if e == 0:
                    wait(act, stored, 16, j, 16)
                for c in range(C):
                    last = nc.scalar.activation(e_out[:, e, c, :], out_bank[c][:, 0:S], ACT.Copy)
                last.then_inc(e_out_done, 1)

            def rest(name, j):
                if name == "aT":
                    wait(act, att_turned, 1, j, 1)
                    wait(act, k_placed, 16 * 6, j, 16 * 6)
                    psum = chunked(pv_bank[0])
                    for c in range(C):
                        last = nc.scalar.activation(ak_hi[:, c, :], psum[:, c, :], ACT.Identity, bias=vec[:, c, BV:BV + 1])
                    last.then_inc(att_hi_done, 1)
                elif name == "wi_part":
                    chosen_hi_part(0, C * F, 1, j)
                elif name[:-1] == "wo_part":
                    n, size = int(name[-1]), C * F // STEPS
                    chosen_hi_part(C * F + n * size, C * F + (n + 1) * size, 2, j)
                elif name[0] == "H":
                    s = int(name[1:])
                    wait(act, hid_filled, LSTEPS, j, s + 1)
                    if s >= 2:
                        wait(act, step_done, LSTEPS, j, s - 1)
                    nc.scalar.activation(hid_hi[:, s % 2, :], hid_bank[s % 2][:, :], ACT.Relu).then_inc(hid_hi_done, 1)
                elif name[0] == "P" and int(name[1:]) % STEPS == STEPS - 1:
                    keep_output(int(name[1:]) // STEPS, j)
                elif name == "logits":
                    wait(act, logits_read, 1, j, 1)
                    nc.scalar.activation(gate_s[:, 4:7], gate_s[:, 1:4], ACT.Exp).then_inc(gate_exp, 1)
                elif name == "x3_parts":
                    wait(act, x3_done, 1, j, 1)
                    nc.scalar.activation(x3_hi[:, :, :], x3T[:, :, :], ACT.Copy).then_inc(x3_hi_done, 1)
                elif name == "sum":
                    wait(act, gate_set, 1, j, 1)
                    for e in (0, 1):
                        n = 9 + (e + 1) % NE
                        nc.scalar.activation(e_out[:, e, :, :], e_out[:, e, :, :], ACT.Copy, scale=gate_s[:, n:n + 1]).then_inc(scaled, 1)

            def stage(name, seq):
                if name in USE or name in ("x_parts", "w_parts", "s_parts", "x1_parts", "x2_parts", "react"):
                    front(name, seq)
                else:
                    rest(name, seq)

            for i in range(FIRST):
                for name, seq in in_turn(i):
                    if seq == 0 and name == "ks":
                        act.wait_ge(consts_set, 3)
                    stage(name, seq)
                    if seq == 0 and name in SHARED_AT:
                        shared_hi_part(SHARED_AT.index(name))
            with act.Fori(FIRST, LAST) as i:
                for name, seq in in_turn(i):
                    stage(name, seq)
            for i in range(LAST, B + 2):
                for name, seq in in_turn(i):
                    stage(name, seq)

        @block.vector
        def _(dve):
            link_sems = {"early": early_link, "attention": attention_link, "rest": rest_link}
            linked = dict.fromkeys(LINKS, 0)

            def link(ins, stretch, seq):
                linked[stretch] += 1
                ins.then_inc(link_sems[stretch], 1)
                wait(dve, link_sems[stretch], LINKS[stretch], seq, linked[stretch])

            def lo_part(i, name, hi, lo, bias=None):
                wait(dve, hi_done, NHI, i, HI_OF[name])
                psum = chunked(front_psum(name))
                if bias is None:
                    return nc.vector.tensor_tensor(lo[:, :, :], psum, hi[:, :, :].bitcast(F32), ALU.subtract)
                for c in range(C):
                    last = nc.vector.scalar_tensor_tensor(lo[:, c, :], psum[:, c, :], bias[:, c:c + 1],
                                                          hi[:, c, :].bitcast(F32), ALU.add, ALU.subtract)
                return last

            def front(name, i):
                def linkf(ins):
                    link(ins, "early" if name in EARLY + ["x_parts", "react"] else "attention", i)

                def rest_of(src, hi, lo):
                    return nc.vector.tensor_tensor(lo[:, :, :], src[:, :, :], hi[:, :, :].bitcast(F32), ALU.subtract)

                psum = chunked(front_psum(name)) if name in USE else None
                if name == "x_parts":
                    wait(dve, small_in, 32, i, 32)
                    nc.vector.tensor_scalar(z_neg[:, :], z_sb[:, 2:3], -1.0, None, ALU.mult)
                    linkf(nc.vector.scalar_tensor_tensor(z_mid[:, :], z_sb[:, 1:2], -2.0, z_sb[:, 2:3], ALU.mult, ALU.add))
                    nc.vector.tensor_scalar(z_mid[:, :], z_mid[:, :], 1.0, None, ALU.add)
                elif name == "x1":
                    wait_filled(dve, i, name)
                    for c in range(C):
                        last = nc.vector.scalar_tensor_tensor(x1T[:, c, :], psum[:, c, :], b0_sb[:, c:c + 1], x_raw[:, c, :],
                                                              ALU.add, ALU.add)
                    last.then_inc(freed_dve, 1)
                elif name == "x1_parts":
                    wait(dve, x1_hi, 1, i, 1)
                    rest_of(x1T, x_hi, x_lo).then_inc(x1_split, 1)
                elif name == "react":
                    wait(dve, react_done, 1, i, 1)
                    linkf(nc.vector.tensor_tensor(react[:, :, :], react[:, :, :], x1T[:, :, :], ALU.mult))
                    wait(dve, beside_done, 1, i, 1)
                    linkf(nc.vector.scalar_tensor_tensor(react[:, :, :], beside[:, :, :], z_sb[:, 1:2], react[:, :, :],
                                                         ALU.mult, ALU.add))
                elif name == "lap":
                    wait_filled(dve, i, name)
                    nc.vector.scalar_tensor_tensor(react[:, :, :], psum, z_sb[:, 0:1], react[:, :, :],
                                                   ALU.mult, ALU.add).then_inc(freed_dve, 1)
                elif name == "x2_parts":
                    wait(dve, x2_hi, 1, i, 1)
                    rest_of(react, x_hi, x_lo).then_inc(x2_split, 1)
                elif name == "self":
                    wait(dve, self_done, 1, i, 1)
                    nc.vector.tensor_copy(s_self[:, :, :], pv_bank[0][:, 0:C * H].rearrange("p (t h) -> p t h", h=H))
                elif name == "kp":
                    lo_part(i, name, ak_hi, ak_lo, ebias[:, 2, :]).then_inc(freed_dve, 1)
                elif name == "vp":
                    wait(dve, v_hi, 1, i, 1)
                    for t in range(C):
                        v = psum[:, t, :].rearrange("p (h d) -> p h d", d=DH)
                        first, second = (v_cols[:, t, :, n * DH:(n + 1) * DH] for n in range(2))
                        nc.vector.tensor_tensor(v_rest[:, t, :].rearrange("p (h d) -> p h d", d=DH), v, first, ALU.subtract)
                        last = nc.vector.tensor_tensor(second, v, first, ALU.subtract)
                    last.then_inc(freed_dve, 1)
                    for c in range(C):
                        nc.vector.tensor_scalar(x2b[:, c, :], react[:, c, :], vec[:, c, BO:BO + 1], None, ALU.add)
                elif name[0] == "S":
                    h = int(name[1:])
                    wait_filled(dve, i, name)
                    nc.vector.tensor_reduce(s_max[:, :, h:h + 1], psum, AX_X, ALU.max).then_inc(freed_dve, 1)
                    if h == H - 1:
                        wait_freed_dve(dve, i, name)
                        nc.vector.tensor_tensor(s_max[:, :, :], s_max[:, :, :], s_self[:, :, :], ALU.max).then_inc(max_done, 1)
                        wait(dve, max_done, 1, i, 1)
                        nc.vector.tensor_tensor(d_self[:, :, :], s_self[:, :, :], s_max[:, :, :], ALU.subtract
                                                ).then_inc(d_self_done, 1)
                elif name == "mT":
                    wait_filled(dve, i, name)
                    rows = front_psum(name)[0:H, 0:S]
                    linkf(nc.vector.tensor_scalar(max_rows[:, 0, :], rows, -1.0, None, ALU.mult))
                    nc.vector.scalar_tensor_tensor(max_rows[:, 1, :], rows, -1.0, max_rows[:, 0, :].bitcast(F32),
                                                   ALU.mult, ALU.subtract).then_inc(freed_dve, 1)
                if name[0] == "E" and int(name[1:]) in DVE_PARTS:
                    h = int(name[1:])
                    wait_freed_act(dve, i, name)
                    if h >= NPROB:
                        wait(dve, pv_done, H, i, h - NPROB + 1)
                    linkf(nc.vector.tensor_copy(prob_hi[:, h % NPROB, :], prob[:, h % NPROB, :]))
                    nc.vector.tensor_tensor(prob_lo[:, h % NPROB, :], prob[:, h % NPROB, :], prob_hi[:, h % NPROB, :],
                                            ALU.subtract).then_inc(prob_split_dve, 1)
                if name in ("half", "att"):
                    half = 0 if name == "half" else 1
                    wait(dve, pv_done, H, i, HALF * (half + 1))
                    wait(dve, p_self_done, 1, i, 1)
                    heads = slice(HALF * half, HALF * (half + 1))
                    cols = slice(HALF * DH * half, HALF * DH * (half + 1))
                    for t in range(C):
                        sums = pv_bank[t][:, 0:HALF * VW].rearrange("p (h w) -> p h w", w=VW)
                        nc.vector.tensor_reduce(att[:, t, cols].rearrange("p (h d) -> p h d", d=DH),
                                                sums[:, :, 0:3 * DH].rearrange("p h (g d) -> p h d g", g=3), AX_X, ALU.add)
                        nc.vector.tensor_tensor(den[:, t, heads], sums[:, :, 3 * DH], p_self[:, t, heads], ALU.add).then_inc(pv_freed, 1)
                if name in ("norm", "att"):
                    half = 0 if name == "norm" else 1
                    heads = slice(HALF * half, HALF * (half + 1))
                    cols = slice(HALF * DH * half, HALF * DH * (half + 1))
                    wait(dve, pv_freed, 2 * C, i, C * (half + 1))
                    wait(dve, own_done, 1, i, 1)
                    nc.vector.tensor_tensor(att[:, :, cols], att[:, :, cols], v_self[:, :, cols], ALU.add)
                    linkf(nc.vector.reciprocal(den[:, :, heads], den[:, :, heads]))
                    for t in range(C):
                        by_head = att[:, t, cols].rearrange("p (h d) -> p h d", d=DH)
                        last = nc.vector.tensor_tensor(by_head, by_head, den[:, t, heads].unsqueeze(2).to_broadcast([P, HALF, DH]),
                                                       ALU.mult)
                    if half == 1:
                        last.then_inc(att_done, 1)

            def rest(name, j):
                def linke(ins):
                    link(ins, "rest", j)

                if name == "aT":
                    wait(dve, att_hi_done, 1, j, 1)
                    psum = chunked(pv_bank[0])
                    for c in range(C):
                        last = nc.vector.scalar_tensor_tensor(ak_lo[:, c, :], psum[:, c, :], vec[:, c, BV:BV + 1],
                                                              ak_hi[:, c, :].bitcast(F32), ALU.add, ALU.subtract)
                    last.then_inc(att_split, 1)
                elif name == "scale":
                    wait(dve, gate_set, 1, j, 1)
                    y = e_out[:, CHOSEN, :, :]
                    nc.vector.scalar_tensor_tensor(y, y, gate_s[:, 9:10], x3T[:, :, :], ALU.mult, ALU.add).then_inc(chosen_added, 1)
                elif name == "wo":
                    wait(dve, wo_done, 1, j, 1)
                    wait(dve, chosen_added, 1, j, 0)
                    nc.vector.tensor_tensor(x3T[:, :, :], chunked(pv_bank[1]), x2b[:, :, :], ALU.add).then_inc(x3_done, 1)
                elif name == "x3_parts":
                    wait(dve, x3_hi_done, 1, j, 1)
                    nc.vector.tensor_tensor(x3_lo[:, :, :], x3T[:, :, :], x3_hi[:, :, :].bitcast(F32), ALU.subtract).then_inc(x3_split, 1)
                elif name[0] == "H":
                    s = int(name[1:])
                    wait(dve, hid_hi_done, LSTEPS, j, s + 1)
                    nc.vector.scalar_tensor_tensor(hid_lo[:, s % 2, :], hid_bank[s % 2][:, :], 0.0,
                                                   hid_hi[:, s % 2, :].bitcast(F32), ALU.max, ALU.subtract).then_inc(hid_split, 1)
                elif name[:-1] == "gate":
                    e = int(name[-1])
                    wait(dve, e_out_done, NE, j, e + 1)
                    if e == 0:
                        dve.wait_ge(gate_in, 32)
                    for k in range(C):
                        w, y = gate1[:, (e + 1) % NE * C + k, :], e_out[:, e, k, 0:1]
                        if (e, k) == (0, 0):
                            linke(nc.vector.tensor_scalar(gate_terms[:, :], w, y, None, ALU.mult))
                        elif (e, k) == (NE - 1, C - 1):
                            nc.vector.scalar_tensor_tensor(gate_terms[:, :], w, y, gate_terms[:, :], ALU.mult, ALU.add
                                                           ).then_inc(gate_terms_done, 1)
                        else:
                            linke(nc.vector.scalar_tensor_tensor(gate_terms[:, :], w, y, gate_terms[:, :], ALU.mult, ALU.add))
                elif name == "relu":
                    wait(dve, gate_done, 1, j, 1)
                    for c in range(C):
                        last = nc.vector.tensor_scalar(gate_h[:, c, :], out_bank[c][:, S:S + 1].to_broadcast([P, P]), 0.0, None, ALU.max)
                    last.then_inc(gate_relu, 1)
                elif name == "logits":
                    wait(dve, logits_done, 1, j, 1)
                    linke(nc.vector.tensor_reduce(gate_s[:, 0:1], out_bank[0][:, 0:3], AX_X, ALU.max))
                    nc.vector.tensor_scalar(gate_s[:, 1:4], out_bank[0][:, 0:3], gate_s[:, 0:1], None, ALU.subtract
                                            ).then_inc(logits_read, 1)
                elif name == "mix":
                    wait(dve, gate_exp, 1, j, 1)
                    linke(nc.vector.tensor_reduce(gate_s[:, 7:8], gate_s[:, 4:7], AX_X, ALU.add))
                    linke(nc.vector.reciprocal(gate_s[:, 8:9], gate_s[:, 7:8]))
                    nc.vector.tensor_scalar(gate_s[:, 9:12], gate_s[:, 4:7], gate_s[:, 8:9], None, ALU.mult).then_inc(gate_set, 1)

            def turn(i):
                linked.update(dict.fromkeys(LINKS, 0))
                for name, seq in in_turn(i, DVE_BODY):
                    if name in USE or name in ("x_parts", "x1_parts", "x2_parts", "react", "self", "half", "norm", "att"):
                        front(name, seq)
                    else:
                        rest(name, seq)
                    if isinstance(i, int) and i == 0 and name == "x1_parts":
                        setup()
                assert all(n in (0, LINKS[stretch]) for stretch, n in linked.items()), linked

            def setup():
                dve.wait_ge(lin_in, 64)
                for n, w in enumerate(LIN_ORDER):
                    cols = slice(w * C * D, (w + 1) * C * D)
                    nc.vector.tensor_copy(lin_hi[:, w, :], raw[:, cols]).then_inc(lin_hi_done, 1)
                    dve.wait_ge(lin_hi_done, n + 1)
                    nc.vector.tensor_tensor(lin_lo[:, w, :], raw[:, cols], lin_hi[:, w, :].bitcast(F32), ALU.subtract
                                            ).then_inc(lin_split, 1)
                dve.wait_ge(consts_in, 16 * 6)
                nc.vector.tensor_copy(lap_mats[:, :], e_out[:, 0, :, :].rearrange("p c t -> p (c t)")).then_inc(consts_set, 1)
                nc.vector.tensor_copy(len_f[:, :], len_sb[:, :]).then_inc(consts_set, 1)
                dve.wait_ge(consts_set, 2)
                nc.vector.tensor_scalar(mask_rows, iota_sb, len_f[:, :], MASKED, ALU.is_ge, ALU.mult).then_inc(mask_set, 1)
                dve.wait_ge(bias_done, 1)
                nc.vector.tensor_tensor(ebias[:, 0, :], pv_bank[0][:, 0:2], vec[:, :, BQ], ALU.add)
                nc.vector.tensor_tensor(ebias[:, 1, :], pv_bank[0][:, 3:6:2], vec[:, :, BK], ALU.add)
                nc.vector.tensor_tensor(ebias[:, 2, :], pv_bank[0][:, 2:6:2], vec[:, :, BK], ALU.add).then_inc(consts_set, 1)
                dve.wait_ge(consts_set, 3)

            for i in range(FIRST):
                turn(i)
            with dve.Fori(FIRST, LAST) as i:
                turn(i)
            for i in range(LAST, B + 2):
                turn(i)

        @block.gpsimd
        def _(pool):
            def split_shared(n):
                to, at = shared_piece(n)
                pool.wait_ge(shared_hi, n + 1)
                nc.gpsimd.tensor_tensor(exp_lo[:, n // 4, to], raw[:, at], exp_hi[:, n // 4, to].bitcast(F32),
                                        ALU.subtract).then_inc(w_split, 1)

            def split_chosen(first, last, n, j):
                wait(pool, chosen_hi, PARTS, j, n)
                at = first % (C * F)
                nc.gpsimd.tensor_tensor(exp_lo[:, CHOSEN, first:last], raw[:, at:at + last - first],
                                        exp_hi[:, CHOSEN, first:last].bitcast(F32), ALU.subtract).then_inc(w_split, 1)

            def stage(name, i):
                first = isinstance(i, int) and i == 0
                if name == "wi_part":
                    split_chosen(0, C * F, 1, i)
                elif name[:-1] == "wo_part":
                    n, size = int(name[-1]), C * F // STEPS
                    split_chosen(C * F + n * size, C * F + (n + 1) * size, 2 + n, i)
                elif name in ("x_parts", "w_parts", "s_parts"):
                    n = ("x_parts", "w_parts", "s_parts").index(name)
                    raw_part, hi, lo = ((x_raw, x_hi, x_lo), (w0_raw, p_hi, p_lo), (s_raw, s_hi, s_lo))[n]
                    wait(pool, in_hi, 3, i, n + 1)
                    nc.gpsimd.tensor_tensor(lo[:, :, :], raw_part[:, :, :], hi[:, :, :].bitcast(F32), ALU.subtract).then_inc(in_split, 1)
                elif name == "x1":
                    wait_freed_dve(pool, i, "x1")
                    nc.gpsimd.tensor_tensor(beside[:, :, 1:S - 1], x1T[:, :, 0:S - 2], x1T[:, :, 2:S], ALU.add)
                    ends = x1T[:, :, 1:S - 1:S - 3]
                    nc.gpsimd.tensor_tensor(beside[:, :, 0:S:S - 1], ends, ends, ALU.add).then_inc(beside_done, 1)
                elif name == "q":
                    wait(pool, hi_done, NHI, i, HI_OF["q"])
                    nc.gpsimd.tensor_tensor(p_lo[:, :, :], q_full[:, :, :], p_hi[:, :, :].bitcast(F32), ALU.subtract).then_inc(q_split, 1)
                elif name == "vs":
                    wait_freed_act(pool, i, "q")
                    nc.gpsimd.tensor_tensor(ksT[:, :, :], ksT[:, :, :], q_full[:, :, :], ALU.mult).then_inc(qk_done, 1)
                elif name == "sum":
                    y = e_out[:, CHOSEN, :, :]
                    wait(pool, scaled, NE - 1, i, NE - 1)
                    wait(pool, chosen_added, 1, i, 1)
                    nc.gpsimd.tensor_tensor(y, y, e_out[:, 0, :, :], ALU.add).then_inc(mix_link, 1)
                    wait(pool, mix_link, 1, i, 1)
                    nc.gpsimd.tensor_tensor(y, y, e_out[:, 1, :, :], ALU.add).then_inc(mixed, 1)
                elif name == "vp":
                    wait_freed_dve(pool, i, "vp")
                    for t in range(C):
                        second, third = (v_cols[:, t, :, n * DH:(n + 1) * DH] for n in (1, 2))
                        last = nc.gpsimd.tensor_tensor(third, v_rest[:, t, :].rearrange("p (h d) -> p h d", d=DH), second, ALU.subtract)
                    last.then_inc(v_split, 1)
                elif name == "mT":
                    wait(pool, p_self_done, 1, i, 1)
                    own = v_self[:, :, :].rearrange("p t (h d) -> p (t h) d", d=DH)
                    nc.gpsimd.tensor_tensor(own, own, p_self[:, :, :].rearrange("p t h -> p (t h)").unsqueeze(2).to_broadcast([P, C * H, DH]),
                                            ALU.mult).then_inc(own_done, 1)
                elif name[0] == "E" and int(name[1:]) not in DVE_PARTS:
                    h = int(name[1:])
                    wait_freed_act(pool, i, name)
                    nc.gpsimd.tensor_tensor(prob_lo[:, h % NPROB, :], prob[:, h % NPROB, :], prob_hi[:, h % NPROB, :],
                                            ALU.subtract).then_inc(prob_split_pool, 1)
                if first and name in SHARED_AT:
                    split_shared(SHARED_AT.index(name))

            nc.gpsimd.memset(q_rows[:, :, :].bitcast(F32), 1.0).then_inc(rows_set, 1)
            nc.gpsimd.memset(k_rows[:, :, :].bitcast(F32), 1.0).then_inc(rows_set, 1)
            nc.gpsimd.memset(v_cols[:, :, :, :], 1.0).then_inc(rows_set, 1)
            nc.gpsimd.memset(ones[:, :], 1.0).then_inc(rows_set, 1)
            pool.wait_ge(rows_set, 4)
            for i in range(FIRST):
                for name, seq in in_turn(i):
                    stage(name, seq)
            with pool.Fori(FIRST, LAST) as i:
                for name, seq in in_turn(i):
                    stage(name, seq)
            for i in range(LAST, B + 2):
                for name, seq in in_turn(i):
                    stage(name, seq)


def kernel(**inputs):
    import concourse.bacc as bacc
    from concourse.bass_utils import run_bass_kernel_spmd as run

    a = {k: np.ascontiguousarray(v) for k, v in inputs.items()}
    order = [8 * c + 4 * e + n for e in range(2) for n in range(4) for c in range(2)]
    v_perm = np.array([h * DH + d for h in order for d in range(DH)])
    qk_perm = np.array([P * c + 64 * e + DH * n + d for c in range(2) for e in range(2) for d in range(DH) for n in range(4)])
    wqkvo = np.stack([a["L2_cond_Wq"][:, qk_perm], a["L2_cond_Wk"][:, qk_perm], a["L2_cond_Wv"][:, v_perm],
                      a["L2_cond_Wo"][v_perm, :]])

    def by_partition(v):
        return v.reshape(C, P).T

    vecs = np.stack([by_partition(v) for v in (a["L2_cond_bq"][qk_perm], a["L2_cond_bk"][qk_perm], a["L2_cond_bo"], a["L2_cond_bv"][v_perm],
                                               a["L2_cond_b_prev"].reshape(D), a["L2_cond_b_self"].reshape(D))], axis=2)
    lap = np.zeros((D, D), np.float32)
    for m in range(D):
        lap[m, m] = -2.0
        for k in (m - 1, m + 1):
            lap[k if 0 <= k < D else 2 * m - k, m] += 1.0
    ones = np.zeros((P, C, H), np.float32)
    for c in range(C):
        for m in range(P):
            ones[m, c, (m // 64) * HALF + 2 * (m % 4) + c] = 1.0
    consts = np.concatenate([np.eye(P, dtype=np.float32), lap[0:P, 0:P], lap[P:, P:], lap[P:, 0:P], lap[0:P, P:],
                             ones.reshape(P, C * H)], axis=1)
    iota = np.tile(np.arange(S, dtype=np.float32), (B, 1))

    arrays = {
        "x": a["x"].transpose(0, 2, 1), "side": a["fside_BxSxS_0"].transpose(0, 2, 1), "seq_len": a["itok_B_18_1004"].reshape(B, 1),
        "subject": a["itok_B_0_7"].reshape(1, B), "label": a["itok_B_0_2"].reshape(1, B),
        "z": np.stack([a["condB_zX"], a["condB_zY"], a["condB_zR"]], axis=1),
        "w0": a["L0_cond_weight"].transpose(0, 2, 1), "b0": a["L0_cond_bias"].reshape(-1, C, P).transpose(0, 2, 1),
        "wqkvo": wqkvo, "vecs": vecs,
        "wi": a["L3_cond_wi"], "wo": a["L3_cond_wo"], "swi": a["L3_cond_swi"], "swo": a["L3_cond_swo"],
        "g1": a["L3_cond_g1"], "g2": a["L3_cond_g2"], "consts": consts, "iota": iota,
    }
    arrays = {f"in_{k}": np.ascontiguousarray(v) for k, v in arrays.items()}
    nc = bacc.Bacc("TRN2", target_bir_lowering=False, num_devices=1, dynamic_dma_scratch_size=1024)
    args = [nc.dram_tensor(k, v.shape, mybir.dt.from_np(v.dtype), kind="ExternalInput").ap() for k, v in arrays.items()]
    out = nc.dram_tensor("out", (B, D, S), F32, kind="ExternalOutput").ap()
    build(nc, *args, out)
    return np.ascontiguousarray(run(nc, [arrays], core_ids=[0]).results[0]["out"].transpose(0, 2, 1))
```
